# Optimizing a Trainium2 kernel written in Bass

```python
import numpy as np
import jax
import jax.numpy as jnp

def _softmax(x, axis=-1):
    return jax.nn.softmax(x, axis=axis)

def _gelu(x):
    return jax.nn.gelu(x, approximate=True)

def _silu(x):
    return jax.nn.silu(x)

def _sigmoid(x):
    return jax.nn.sigmoid(x)

def _layernorm(x, axis=-1, eps=1e-05):
    m = jnp.mean(x, axis=axis, keepdims=True)
    v = jnp.var(x, axis=axis, keepdims=True)
    return (x - m) / jnp.sqrt(v + eps)

def _scatter_add(tgt, idx, src, axis=0):
    return tgt.at[idx].add(src)

def _segment_sum(src, seg, n):
    return jax.ops.segment_sum(src, seg, n)
kernel_name = 'mk_dlrm_tower_d1_rec_r8_9b2d12'

def setup_inputs(seed: int=0):
    np.random.seed(seed)
    _w = jnp.asarray

    def _rec_inputs():
        import jax
        import jax.numpy as jnp
        _tk = jax.random.key(seed)
        dense_ctx = jax.random.normal(jax.random.fold_in(_tk, 190), (1024, 16), jnp.float32)
        ids = jnp.stack([jax.random.randint(jax.random.fold_in(_tk, 200 + f), (1024,), 0, v, jnp.int32) for f, v in enumerate([125000, 12500, 12500, 1250, 125000, 125000, 1000, 125000, 1250, 1250, 1000, 1250, 125000, 12500, 12500, 12500, 1250, 125000, 12500, 12500, 1250, 1000, 125000, 1250, 1000, 125000, 1250, 125000, 1000, 125000, 125000, 1250, 1000, 1250, 1000, 1250, 1250, 1250, 125000])], axis=1)
        tbl_0 = 0.05 * jax.random.normal(jax.random.fold_in(_tk, 500 + 0), (125000, 16), jnp.float32)
        tbl_1 = 0.05 * jax.random.normal(jax.random.fold_in(_tk, 500 + 1), (12500, 16), jnp.float32)
        tbl_2 = 0.05 * jax.random.normal(jax.random.fold_in(_tk, 500 + 2), (12500, 16), jnp.float32)
        tbl_3 = 0.05 * jax.random.normal(jax.random.fold_in(_tk, 500 + 3), (1250, 16), jnp.float32)
        tbl_4 = 0.05 * jax.random.normal(jax.random.fold_in(_tk, 500 + 4), (125000, 16), jnp.float32)
        tbl_5 = 0.05 * jax.random.normal(jax.random.fold_in(_tk, 500 + 5), (125000, 16), jnp.float32)
        tbl_6 = 0.05 * jax.random.normal(jax.random.fold_in(_tk, 500 + 6), (1000, 16), jnp.float32)
        tbl_7 = 0.05 * jax.random.normal(jax.random.fold_in(_tk, 500 + 7), (125000, 16), jnp.float32)
        tbl_8 = 0.05 * jax.random.normal(jax.random.fold_in(_tk, 500 + 8), (1250, 16), jnp.float32)
        tbl_9 = 0.05 * jax.random.normal(jax.random.fold_in(_tk, 500 + 9), (1250, 16), jnp.float32)
        tbl_10 = 0.05 * jax.random.normal(jax.random.fold_in(_tk, 500 + 10), (1000, 16), jnp.float32)
        tbl_11 = 0.05 * jax.random.normal(jax.random.fold_in(_tk, 500 + 11), (1250, 16), jnp.float32)
        tbl_12 = 0.05 * jax.random.normal(jax.random.fold_in(_tk, 500 + 12), (125000, 16), jnp.float32)
        tbl_13 = 0.05 * jax.random.normal(jax.random.fold_in(_tk, 500 + 13), (12500, 16), jnp.float32)
        tbl_14 = 0.05 * jax.random.normal(jax.random.fold_in(_tk, 500 + 14), (12500, 16), jnp.float32)
        tbl_15 = 0.05 * jax.random.normal(jax.random.fold_in(_tk, 500 + 15), (12500, 16), jnp.float32)
        tbl_16 = 0.05 * jax.random.normal(jax.random.fold_in(_tk, 500 + 16), (1250, 16), jnp.float32)
        tbl_17 = 0.05 * jax.random.normal(jax.random.fold_in(_tk, 500 + 17), (125000, 16), jnp.float32)
        tbl_18 = 0.05 * jax.random.normal(jax.random.fold_in(_tk, 500 + 18), (12500, 16), jnp.float32)
        tbl_19 = 0.05 * jax.random.normal(jax.random.fold_in(_tk, 500 + 19), (12500, 16), jnp.float32)
        tbl_20 = 0.05 * jax.random.normal(jax.random.fold_in(_tk, 500 + 20), (1250, 16), jnp.float32)
        tbl_21 = 0.05 * jax.random.normal(jax.random.fold_in(_tk, 500 + 21), (1000, 16), jnp.float32)
        tbl_22 = 0.05 * jax.random.normal(jax.random.fold_in(_tk, 500 + 22), (125000, 16), jnp.float32)
        tbl_23 = 0.05 * jax.random.normal(jax.random.fold_in(_tk, 500 + 23), (1250, 16), jnp.float32)
        tbl_24 = 0.05 * jax.random.normal(jax.random.fold_in(_tk, 500 + 24), (1000, 16), jnp.float32)
        tbl_25 = 0.05 * jax.random.normal(jax.random.fold_in(_tk, 500 + 25), (125000, 16), jnp.float32)
        tbl_26 = 0.05 * jax.random.normal(jax.random.fold_in(_tk, 500 + 26), (1250, 16), jnp.float32)
        tbl_27 = 0.05 * jax.random.normal(jax.random.fold_in(_tk, 500 + 27), (125000, 16), jnp.float32)
        tbl_28 = 0.05 * jax.random.normal(jax.random.fold_in(_tk, 500 + 28), (1000, 16), jnp.float32)
        tbl_29 = 0.05 * jax.random.normal(jax.random.fold_in(_tk, 500 + 29), (125000, 16), jnp.float32)
        tbl_30 = 0.05 * jax.random.normal(jax.random.fold_in(_tk, 500 + 30), (125000, 16), jnp.float32)
        tbl_31 = 0.05 * jax.random.normal(jax.random.fold_in(_tk, 500 + 31), (1250, 16), jnp.float32)
        tbl_32 = 0.05 * jax.random.normal(jax.random.fold_in(_tk, 500 + 32), (1000, 16), jnp.float32)
        tbl_33 = 0.05 * jax.random.normal(jax.random.fold_in(_tk, 500 + 33), (1250, 16), jnp.float32)
        tbl_34 = 0.05 * jax.random.normal(jax.random.fold_in(_tk, 500 + 34), (1000, 16), jnp.float32)
        tbl_35 = 0.05 * jax.random.normal(jax.random.fold_in(_tk, 500 + 35), (1250, 16), jnp.float32)
        tbl_36 = 0.05 * jax.random.normal(jax.random.fold_in(_tk, 500 + 36), (1250, 16), jnp.float32)
        tbl_37 = 0.05 * jax.random.normal(jax.random.fold_in(_tk, 500 + 37), (1250, 16), jnp.float32)
        tbl_38 = 0.05 * jax.random.normal(jax.random.fold_in(_tk, 500 + 38), (125000, 16), jnp.float32)
        _rk = jax.random.fold_in(_tk, 7)
        W_top1 = 0.05 * jax.random.normal(jax.random.fold_in(_tk, 801), (400, 512), jnp.float32)
        W_top2 = 0.0441942 * jax.random.normal(jax.random.fold_in(_tk, 802), (512, 256), jnp.float32)
        W_top3 = 0.0625 * jax.random.normal(jax.random.fold_in(_tk, 803), (256, 1), jnp.float32)
        b_top1 = jnp.zeros((512,), jnp.float32)
        b_top2 = jnp.zeros((256,), jnp.float32)
        return (dense_ctx, ids, tbl_0, tbl_1, tbl_2, tbl_3, tbl_4, tbl_5, tbl_6, tbl_7, tbl_8, tbl_9, tbl_10, tbl_11, tbl_12, tbl_13, tbl_14, tbl_15, tbl_16, tbl_17, tbl_18, tbl_19, tbl_20, tbl_21, tbl_22, tbl_23, tbl_24, tbl_25, tbl_26, tbl_27, tbl_28, tbl_29, tbl_30, tbl_31, tbl_32, tbl_33, tbl_34, tbl_35, tbl_36, tbl_37, tbl_38, W_top1, b_top1, W_top2, b_top2, W_top3)
    dense_ctx, ids, tbl_0, tbl_1, tbl_2, tbl_3, tbl_4, tbl_5, tbl_6, tbl_7, tbl_8, tbl_9, tbl_10, tbl_11, tbl_12, tbl_13, tbl_14, tbl_15, tbl_16, tbl_17, tbl_18, tbl_19, tbl_20, tbl_21, tbl_22, tbl_23, tbl_24, tbl_25, tbl_26, tbl_27, tbl_28, tbl_29, tbl_30, tbl_31, tbl_32, tbl_33, tbl_34, tbl_35, tbl_36, tbl_37, tbl_38, W_top1, b_top1, W_top2, b_top2, W_top3 = _rec_inputs()

    def _L0_rec_setup():
        import jax, jax.numpy as jnp
        import numpy as np
        B, F0, D = (256, 39, 16)
        CROSS = [128, 128, 128]
        key = jax.random.key(seed)
        k0, k1, k2, k3 = jax.random.split(key, 4)
        inputs = jax.random.normal(k0, (B, F0, D), dtype=jnp.float32)
        f0 = jax.random.normal(k1, (F0 * F0, CROSS[0]), dtype=jnp.float32) * 0.05
        f1 = jax.random.normal(k2, (CROSS[0] * F0, CROSS[1]), dtype=jnp.float32) * 0.05
        f2 = jax.random.normal(k3, (CROSS[1] * F0, CROSS[2]), dtype=jnp.float32) * 0.05
        return {'inputs': inputs, 'f0': f0, 'f1': f1, 'f2': f2}
    _L0_rec_all = _L0_rec_setup()
    _L0_rec_in = {k: v for k, v in _L0_rec_all.items() if k in ('f0', 'f1', 'f2')}
    del _L0_rec_all
    return {'dense_ctx': dense_ctx, 'ids': ids, 'tbl_0': tbl_0, 'tbl_1': tbl_1, 'tbl_2': tbl_2, 'tbl_3': tbl_3, 'tbl_4': tbl_4, 'tbl_5': tbl_5, 'tbl_6': tbl_6, 'tbl_7': tbl_7, 'tbl_8': tbl_8, 'tbl_9': tbl_9, 'tbl_10': tbl_10, 'tbl_11': tbl_11, 'tbl_12': tbl_12, 'tbl_13': tbl_13, 'tbl_14': tbl_14, 'tbl_15': tbl_15, 'tbl_16': tbl_16, 'tbl_17': tbl_17, 'tbl_18': tbl_18, 'tbl_19': tbl_19, 'tbl_20': tbl_20, 'tbl_21': tbl_21, 'tbl_22': tbl_22, 'tbl_23': tbl_23, 'tbl_24': tbl_24, 'tbl_25': tbl_25, 'tbl_26': tbl_26, 'tbl_27': tbl_27, 'tbl_28': tbl_28, 'tbl_29': tbl_29, 'tbl_30': tbl_30, 'tbl_31': tbl_31, 'tbl_32': tbl_32, 'tbl_33': tbl_33, 'tbl_34': tbl_34, 'tbl_35': tbl_35, 'tbl_36': tbl_36, 'tbl_37': tbl_37, 'tbl_38': tbl_38, 'W_top1': W_top1, 'b_top1': b_top1, 'W_top2': W_top2, 'b_top2': b_top2, 'W_top3': W_top3, 'L0_rec_f0': _L0_rec_in['f0'], 'L0_rec_f1': _L0_rec_in['f1'], 'L0_rec_f2': _L0_rec_in['f2']}

def reference(dense_ctx, ids, tbl_0, tbl_1, tbl_2, tbl_3, tbl_4, tbl_5, tbl_6, tbl_7, tbl_8, tbl_9, tbl_10, tbl_11, tbl_12, tbl_13, tbl_14, tbl_15, tbl_16, tbl_17, tbl_18, tbl_19, tbl_20, tbl_21, tbl_22, tbl_23, tbl_24, tbl_25, tbl_26, tbl_27, tbl_28, tbl_29, tbl_30, tbl_31, tbl_32, tbl_33, tbl_34, tbl_35, tbl_36, tbl_37, tbl_38, W_top1, b_top1, W_top2, b_top2, W_top3, L0_rec_f0, L0_rec_f1, L0_rec_f2):
    import jax
    import jax.numpy as jnp

    def _L0_rec_ref(inputs, f0, f1, f2):
        import jax, jax.numpy as jnp
        import numpy as np
        B, F0, D = (256, 39, 16)
        CROSS = [128, 128, 128]
        filters = [f0, f1, f2]
        x0 = inputs
        xk = inputs
        outs = []
        for W in filters:
            b, f, d = x0.shape
            g = xk.shape[1]
            z = jnp.einsum('bfd,bgd->bfgd', x0, xk).reshape(b, f * g, d)
            cur = jnp.einsum('bpd,pm->bmd', z, W)
            outs.append(cur)
            xk = cur
        result = jnp.concatenate(outs, axis=1)
        return jnp.sum(result, axis=-1)
    e = jnp.stack([tbl_0[ids[:, 0]], tbl_1[ids[:, 1]], tbl_2[ids[:, 2]], tbl_3[ids[:, 3]], tbl_4[ids[:, 4]], tbl_5[ids[:, 5]], tbl_6[ids[:, 6]], tbl_7[ids[:, 7]], tbl_8[ids[:, 8]], tbl_9[ids[:, 9]], tbl_10[ids[:, 10]], tbl_11[ids[:, 11]], tbl_12[ids[:, 12]], tbl_13[ids[:, 13]], tbl_14[ids[:, 14]], tbl_15[ids[:, 15]], tbl_16[ids[:, 16]], tbl_17[ids[:, 17]], tbl_18[ids[:, 18]], tbl_19[ids[:, 19]], tbl_20[ids[:, 20]], tbl_21[ids[:, 21]], tbl_22[ids[:, 22]], tbl_23[ids[:, 23]], tbl_24[ids[:, 24]], tbl_25[ids[:, 25]], tbl_26[ids[:, 26]], tbl_27[ids[:, 27]], tbl_28[ids[:, 28]], tbl_29[ids[:, 29]], tbl_30[ids[:, 30]], tbl_31[ids[:, 31]], tbl_32[ids[:, 32]], tbl_33[ids[:, 33]], tbl_34[ids[:, 34]], tbl_35[ids[:, 35]], tbl_36[ids[:, 36]], tbl_37[ids[:, 37]], tbl_38[ids[:, 38]]], axis=1)
    z = _L0_rec_ref(e, L0_rec_f0, L0_rec_f1, L0_rec_f2)
    z = z.reshape(z.shape[0], -1)
    h = jnp.concatenate([z, dense_ctx], axis=1)
    h = jnp.maximum(h @ W_top1 + b_top1, 0.0)
    h = jnp.maximum(h @ W_top2 + b_top2, 0.0)
    y = h @ W_top3
    return y

_drawn_inputs = setup_inputs


def setup_inputs(seed=0):
    import zlib

    import numpy as np

    out = dict(_drawn_inputs(seed))
    spreads = {'b_top1': (0.0, 0.629), 'b_top2': (0.0, 0.28)}
    factors = {'tbl_0': 4.555,
     'tbl_1': 4.896,
     'tbl_2': 4.772,
     'tbl_3': 4.852,
     'tbl_4': 4.73,
     'tbl_5': 4.771,
     'tbl_6': 4.645,
     'tbl_7': 4.877,
     'tbl_8': 5.333,
     'tbl_9': 4.463,
     'tbl_10': 4.718,
     'tbl_11': 4.601,
     'tbl_12': 4.418,
     'tbl_13': 4.352,
     'tbl_14': 4.761,
     'tbl_15': 4.735,
     'tbl_16': 4.985,
     'tbl_17': 4.63,
     'tbl_18': 5.049,
     'tbl_19': 5.21,
     'tbl_20': 4.81,
     'tbl_21': 4.876,
     'tbl_22': 4.576,
     'tbl_23': 4.938,
     'tbl_24': 4.635,
     'tbl_25': 4.384,
     'tbl_26': 4.86,
     'tbl_27': 5.084,
     'tbl_28': 4.509,
     'tbl_29': 4.705,
     'tbl_30': 4.906,
     'tbl_31': 4.504,
     'tbl_32': 4.793,
     'tbl_33': 4.561,
     'tbl_34': 4.58,
     'tbl_35': 4.609,
     'tbl_36': 4.928,
     'tbl_37': 4.828,
     'tbl_38': 4.994,
     'L0_rec_f1': 5.427,
     'L0_rec_f2': 8.0}
    for name, (base, spread) in spreads.items():
        noise = np.random.default_rng([zlib.crc32(name.encode()), seed]).standard_normal(out[name].shape)
        drawn = base * np.exp(spread * noise) if base else spread * noise
        out[name] = jnp.asarray(drawn.astype(out[name].dtype))
    for name, factor in factors.items():
        out[name] = (out[name] * factor).astype(out[name].dtype)
    return out
```

```python
from contextlib import ExitStack

import concourse.bass as bass
from concourse import mybir

F32 = mybir.dt.float32
F32R = mybir.dt.float32r
BF16 = mybir.dt.bfloat16
I32 = mybir.dt.int32
U32 = mybir.dt.uint32
ALU = mybir.AluOpType
ACT = mybir.ActivationFunctionType
AX_X = mybir.AxisListType.X

P = 128
FIELDS = 39
DIM = 16
BATCH = 1024
TILES = BATCH // P
CHUNK_B = 32
CHUNKS = P // CHUNK_B
N = CHUNK_B * DIM
QUADS = 4
QP = P // QUADS
SLOTS = -(-FIELDS // QUADS)
TSLOTS = CHUNKS * SLOTS
LAST_P = (FIELDS - QUADS * (SLOTS - 1)) * QP
DELTAS = 3
ROWS = DELTAS * FIELDS
PAIRS = 7
LAST_ROWS = (20 - DELTAS * (PAIRS - 1)) * FIELDS
RING = 4
UB = 8
UNITS = P // UB
UG = 4
FC = FIELDS + 1
HID1, HID2, CTX = 512, 256, 16
POOL_COLS = 1024
SPLIT_SLOT = 24
GATHER_SLOT = 26
EARLY = TSLOTS - GATHER_SLOT
LATE = FIELDS - EARLY
LAND = 16
REPS = QUADS * 4


def build(nc, t_ids, t_tables, t_ctx, t_wu, t_wl, t_w1, t_w2, t_top1, t_b1, t_top2, t_b2, t_top3,
          t_sel, t_ident, t_mask, t_out):
    with ExitStack() as ctx:
        def sb(name, shape, dt=F32):
            return ctx.enter_context(nc.sbuf_tensor(name, shape, dt))

        def bank(name):
            return ctx.enter_context(nc.psum_tensor(name, [P, 512], F32))

        def sem(name):
            return ctx.enter_context(nc.semaphore(name))

        ident = sb("ident", [P, P])
        ident_bf = sb("ident_bf", [P, P], BF16)
        mask = sb("mask", [P, UB])
        spread = sb("spread", [ROWS, SLOTS, P], BF16)
        pairsel = sb("pairsel", [ROWS, 1 + PAIRS, ROWS], BF16)
        joinsel = sb("joinsel", [ROWS, FIELDS], BF16)
        ws = sb("ws", [ROWS, PAIRS, P])
        wh = sb("wh", [P, SLOTS, 4, P], F32R)
        wl = sb("wl", [P, SLOTS, 4, P], F32R)
        w2 = sb("w2", [P, FIELDS, P])
        top1 = sb("top1", [P, 3, HID1])
        top1c = sb("top1c", [CTX, HID1])
        top2 = sb("top2", [P, HID1 // P, HID2])
        top3 = sb("top3", [P, HID2 // P])
        b1 = sb("b1", [P, HID1 // P])
        b2 = sb("b2", [P, HID2 // P])
        ids_early = sb("ids_early", [P, EARLY], I32)
        ids_late = sb("ids_late", [P, LATE], I32)
        emb = sb("emb", [P, FIELDS, DIM])
        parts = sb("parts", [P, DIM, ROWS], BF16)
        x0t = sb("x0t", [ROWS, CHUNKS, N], BF16)
        xa = sb("xa", [ROWS, N])
        z1 = sb("z1", [ROWS, RING, N])
        x1 = sb("x1", [P, N])
        x1q = sb("x1q", [P, 2, 4, N])
        z = sb("z", [P, 2, 4 * N])
        z_flat = z[:, :, :].rearrange("p a n -> p (a n)")
        zh = sb("zh", [P, 2, 4 * N], F32R)
        zl = sb("zl", [P, 2, 4 * N], F32R)
        x2 = sb("x2", [P, P * DIM])
        x2t = sb("x2t", [P, UNITS, P])
        xn = sb("xn", [P, UNITS, FIELDS])
        diag = sb("diag", [P, 2, FC, UB])
        gram = sb("gram", [P, FC, P])
        sum1_next = sb("sum1_next", [P, P])
        sum1 = sb("sum1", [P, P])
        sum3 = sb("sum3", [P, P])
        ctxt = sb("ctxt", [CTX, P])
        h1 = sb("h1", [P, HID1 // P, P])
        h2 = sb("h2", [P, HID2 // P, P])
        y = sb("y", [1, P])

        ps_tail = bank("ps_tail")
        ps_spread = [bank("ps_spread0"), bank("ps_spread1")]
        ps_front = [bank("ps_front0"), bank("ps_front1")]
        ps_l1 = bank("ps_l1")
        ps_l2 = [bank("ps_l2a"), bank("ps_l2b")]

        s_ids0 = sem("s_ids0")
        s_sel = sem("s_sel")
        s_w0 = sem("s_w0")
        s_w1 = sem("s_w1")
        s_w2 = sem("s_w2")
        s_top = sem("s_top")
        s_ids_early = sem("s_ids_early")
        s_ids_late = sem("s_ids_late")
        s_ctx = sem("s_ctx")
        s_emb_early = sem("s_emb_early")
        s_emb_late = sem("s_emb_late")
        s_x1q = sem("s_x1q")
        s_out = sem("s_out")
        s_consts = sem("s_consts")
        s_wh = sem("s_wh")
        s_ws = sem("s_ws")
        s_wl = sem("s_wl")
        s_hi = sem("s_hi")
        s_rest = sem("s_rest")
        s_mid = sem("s_mid")
        s_parts = sem("s_parts")
        s_x0_ps = sem("s_x0_ps")
        s_x0t = sem("s_x0t")
        s_xa_ps = sem("s_xa_ps")
        s_xa = sem("s_xa")
        s_pair_ps = sem("s_pair_ps")
        s_z1 = sem("s_z1")
        s_l1 = sem("s_l1")
        s_x1 = sem("s_x1")
        s_sums = sem("s_sums")
        s_sum1 = sem("s_sum1")
        s_spread = sem("s_spread")
        s_z = sem("s_z")
        s_zh = sem("s_zh")
        s_zl_dve = sem("s_zl_dve")
        s_zl_pool = sem("s_zl_pool")
        s_l2 = sem("s_l2")
        s_x2 = sem("s_x2")
        s_xn_ps = sem("s_xn_ps")
        s_xn = sem("s_xn")
        s_x2t_ps = sem("s_x2t_ps")
        s_x2t = sem("s_x2t")
        s_diag = sem("s_diag")
        s_gram_ps = sem("s_gram_ps")
        s_gram = sem("s_gram")
        s_l3 = sem("s_l3")
        s_sum3 = sem("s_sum3")
        s_h1_ps = sem("s_h1_ps")
        s_h1 = sem("s_h1")
        s_h2_ps = sem("s_h2_ps")
        s_h2 = sem("s_h2")
        s_y_ps = sem("s_y_ps")
        s_y = sem("s_y")

        block = ctx.enter_context(nc.Block())

        def wait(eng, s, count):
            if isinstance(count, int) and count <= 0:
                return
            eng.wait_ge(s, count)

        def front_at(c, k):
            ahead = c + (2 if k >= SLOTS - 3 else 1)
            return ahead // CHUNKS, ahead % CHUNKS, (k + 3) % SLOTS

        def rows_of(i):
            return LAST_ROWS if i == PAIRS - 1 else ROWS

        def parts_of(k):
            return LAST_P if k == SLOTS - 1 else P

        ids_t = t_ids.rearrange("(t p) f -> t p f", p=P)
        out_t = t_out.rearrange("(t p) o -> t o p", p=P)

        @block.sync
        def _(sp):
            def spread_x1(t, c):
                sp.wait_ge(s_x1, CHUNKS * t + c + 1)
                for j in range(4):
                    for q in range(QUADS):
                        sp.dma_start(x1q[QP * q:QP * q + QP, c % 2, j, :],
                                     x1[QP * j:QP * j + QP, :]).then_inc(s_x1q, LAND)

            sp.dma_start(ids_early[:, :], ids_t[0, :, 0:EARLY]).then_inc(s_ids_early, LAND)
            sp.dma_start(ids_late[:, :], ids_t[0, :, EARLY:FIELDS]).then_inc(s_ids_late, LAND)
            sp.dma_start(z_flat[0:ROWS, 0:t_sel.shape[1]], t_sel).then_inc(s_sel, LAND)
            sp.dma_start(ident[:, :], t_ident).then_inc(s_sel, LAND)
            sp.dma_start(mask[:, :], t_mask).then_inc(s_sel, LAND)
            sp.dma_start(ws[:, :, :], t_wu).then_inc(s_w0, LAND)
            sp.dma_start(x2[0:ROWS, 0:PAIRS * P], t_wl.rearrange("p i m -> p (i m)")).then_inc(s_w0, LAND)
            sp.dma_start(gram[:, :, :], t_w1[:, 0:SLOTS * 4, :]).then_inc(s_w1, LAND)
            sp.dma_start(w2[:, :, :], t_w2).then_inc(s_w2, LAND)
            for dst, src in ((top1[:, :, :], t_top1[0:3 * P, :].rearrange("(k p) n -> p k n", p=P)),
                             (top1c[:, :], t_top1[3 * P:3 * P + CTX, :]),
                             (top2[:, :, :], t_top2.rearrange("(k p) n -> p k n", p=P)),
                             (top3[:, :], t_top3), (b1[:, :], t_b1), (b2[:, :], t_b2)):
                sp.dma_start(dst, src).then_inc(s_top, LAND)
            spread_x1(0, 0)
            with sp.Fori(0, TILES - 1) as t:
                spread_x1(t, 1)
                spread_x1(t, 2)
                spread_x1(t, 3)
                spread_x1(t + 1, 0)
            for c in range(1, CHUNKS):
                spread_x1(TILES - 1, c)

        @block.gpsimd
        def _(pool):
            def gather(t, f):
                ids, at, landed = ((ids_early, f, s_emb_early) if f < EARLY else
                                   (ids_late, f - EARLY, s_emb_late))
                pool.indirect_dma_start(
                    emb[:, f, :], None, t_tables[f],
                    bass.IndirectOffsetOnAxis(ap=ids[:, at:at + 1].bitcast(U32), axis=0),
                ).then_inc(landed, LAND)

            def may_gather(t, late):
                if late:
                    pool.wait_ge(s_ids_late, LAND * (t + 1))
                else:
                    pool.wait_ge(s_ids_early, LAND * (t + 1))
                    wait(pool, s_parts, t)

            def rest(t, u):
                j = TSLOTS * t + u
                pool.wait_ge(s_zh, j + 1)
                wait(pool, s_l2, j - 1)
                p = parts_of(u % SLOTS)
                nc.gpsimd.tensor_tensor(zl[0:p, u % 2, 0:POOL_COLS], z[0:p, u % 2, 0:POOL_COLS],
                                        zh[0:p, u % 2, 0:POOL_COLS].bitcast(F32),
                                        ALU.subtract).then_inc(s_zl_pool, 1)

            def tile(t, near=True, far=True):
                for u in range(TSLOTS):
                    if near and u == 0:
                        may_gather(t + 1, late=True)
                    if far and u == GATHER_SLOT:
                        may_gather(t + 2, late=False)
                    rest(t, u)
                    if near and u < LATE:
                        gather(t + 1, EARLY + u)
                    if far and u >= GATHER_SLOT:
                        gather(t + 2, u - GATHER_SLOT)

            may_gather(0, late=False)
            for f in range(EARLY):
                gather(0, f)
            may_gather(0, late=True)
            for f in range(EARLY, FIELDS):
                gather(0, f)
            may_gather(1, late=False)
            for f in range(EARLY):
                gather(1, f)
            tile(0)
            with pool.Fori(1, TILES - 2) as t:
                tile(t)
            tile(TILES - 2, far=False)
            tile(TILES - 1, near=False, far=False)

        @block.tensor
        def _(pe):
            def front_before(t, c, r):
                g = CHUNKS * t + c
                if r == 0:
                    if c == 0:
                        pe.wait_ge(s_parts, t + 1)
                    wait(pe, s_z1, PAIRS * g)
                    for i in range(DIM):
                        mm = nc.tensor.matmul(
                            ps_front[1][0:ROWS, CHUNK_B * i:CHUNK_B * i + CHUNK_B],
                            parts[:, i, :], ident_bf[:, CHUNK_B * c:CHUNK_B * c + CHUNK_B],
                            start=True, stop=True)
                    mm.then_inc(s_x0_ps, 1)
                if r == 1:
                    pe.wait_ge(s_x0t, g + 1)
                    wait(pe, s_z1, PAIRS * g - 1)
                    if c == 0:
                        wait(pe, s_xn, 2 * t)
                    nc.tensor.matmul(ps_front[0][0:ROWS, :], pairsel[:, 0, :], x0t[:, c, :],
                                     start=True, stop=True).then_inc(s_xa_ps, 1)
                for i in {1: [0], 2: [1, 2], 3: [3, 4], 4: [5, 6]}.get(r, []):
                    if i == 1:
                        pe.wait_ge(s_xa, g + 1)
                    if i >= 2:
                        pe.wait_ge(s_z1, PAIRS * g + i - 1)
                    n = rows_of(i)
                    nc.tensor.matmul(ps_front[(i + 1) % 2][0:n, :], pairsel[:, 1 + i, 0:n],
                                     x0t[:, c, :], start=True, stop=True).then_inc(s_pair_ps, 1)

            def front_after(t, c, r):
                g = CHUNKS * t + c
                for i in {2: [0], 3: [1, 2], 4: [3, 4], 5: [5, 6]}.get(r, []):
                    if i == 0:
                        wait(pe, s_x1, g)
                    pe.wait_ge(s_z1, PAIRS * g + i + 1)
                    n = rows_of(i)
                    nc.tensor.matmul(ps_l1[:, :], ws[0:n, i, :], z1[0:n, i % RING, :],
                                     start=(i == 0), stop=(i == PAIRS - 1)).then_inc(s_l1, 1)

            def fields_of_units(t, half):
                if half == 0:
                    pe.wait_ge(s_x0t, CHUNKS * t + CHUNKS)
                    pe.wait_ge(s_z1, PAIRS * (CHUNKS * t + CHUNKS) - 1)
                else:
                    pe.wait_ge(s_xn, 2 * t + 1)
                units = x0t[:, :, :].rearrange("p c n -> p (c n)")
                for i in range(UNITS // 2):
                    s = UNITS // 2 * half + i
                    mm = nc.tensor.matmul(ps_front[0][:, FIELDS * i:FIELDS * i + FIELDS],
                                          units[:, P * s:P * s + P], joinsel[:, :],
                                          start=True, stop=True)
                mm.then_inc(s_xn_ps, 1)

            def spread_x0(t, c, k):
                j = TSLOTS * t + SLOTS * c + k
                if k == 0:
                    pe.wait_ge(s_x0t, CHUNKS * t + c + 1)
                wait(pe, s_z, j - 1)
                p = parts_of(k)
                nc.tensor.matmul(ps_spread[k % 2][0:p, :], spread[:, k, 0:p], x0t[:, c, :],
                                 start=True, stop=True).then_inc(s_spread, 1)

            def layer2(t, c, k):
                j = TSLOTS * t + SLOTS * c + k
                if k == 0:
                    wait(pe, s_x2, CHUNKS * t + c - 1)
                pe.wait_ge(s_zh, j + 1)
                pe.wait_ge(s_zl_dve, j + 1)
                pe.wait_ge(s_zl_pool, j + 1)
                p = parts_of(k)
                for i in range(4):
                    cols = slice(N * i, N * i + N)
                    for n, (w, x) in enumerate(((wh, zh), (wh, zl), (wl, zh))):
                        mm = nc.tensor.matmul(ps_l2[c % 2][:, :], w[0:p, k, i, :],
                                              x[0:p, k % 2, cols],
                                              start=(k == 0 and i == 0 and n == 0),
                                              stop=(k == SLOTS - 1 and i == 3 and n == 2))
                mm.then_inc(s_l2, 1)

            def tail(t, u):
                if 1 <= u <= UNITS // UG:
                    r = u - 1
                    if r == 0:
                        pe.wait_ge(s_x2, CHUNKS * t)
                    else:
                        pe.wait_ge(s_x2t, UNITS // UG * (t - 1) + r)
                    for i in range(UG):
                        s = UG * r + i
                        mm = nc.tensor.transpose(ps_tail[:, P * i:P * i + P],
                                                 x2[:, P * s:P * s + P], ident[:, :])
                    mm.then_inc(s_x2t_ps, 1)
                if 6 <= u < 6 + UNITS:
                    s = u - 6
                    if s % UG == 0:
                        pe.wait_ge(s_x2t, UNITS // UG * (t - 1) + max(s // UG + 1, UNITS // UG if s == 0 else 0))
                    if s:
                        pe.wait_ge(s_gram, UNITS * (t - 1) + s)
                    pe.wait_ge(s_diag, UNITS * (t - 1) + s + 1)
                    nc.tensor.matmul(ps_tail[:, 0:FC * UB], x2t[:, s, :],
                                     diag[:, s % 2, :, :].rearrange("p f b -> p (f b)"),
                                     start=True, stop=True).then_inc(s_gram_ps, 1)
                if 22 <= u <= 31:
                    if u == 22:
                        pe.wait_ge(s_gram, UNITS * t)
                    for f in range(4 * (u - 22), min(4 * (u - 22) + 4, FIELDS)):
                        mm = nc.tensor.matmul(ps_tail[:, 0:P], w2[:, f, :], gram[:, f, :],
                                              start=(f == 0), stop=(f == FIELDS - 1))
                    if u == 31:
                        mm.then_inc(s_l3, 1)
                if u == 33:
                    pe.wait_ge(s_sum3, t)
                    pe.wait_ge(s_sum1, t)
                    pe.wait_ge(s_ctx, LAND * t)
                    for m in range(HID1 // P):
                        cols = slice(P * m, P * m + P)
                        for n, (w, x) in enumerate(((top1[:, 0, cols], sum1[:, :]),
                                                    (top1[:, 1, cols], gram[:, FIELDS, :]),
                                                    (top1[:, 2, cols], sum3[:, :]),
                                                    (top1c[:, cols], ctxt[:, :]))):
                            mm = nc.tensor.matmul(ps_tail[:, cols], w, x, start=(n == 0),
                                                  stop=(n == 3))
                    mm.then_inc(s_h1_ps, 1)
                if u == 35:
                    pe.wait_ge(s_h1, t)
                    for m in range(HID2 // P):
                        cols = slice(P * m, P * m + P)
                        for n in range(HID1 // P):
                            mm = nc.tensor.matmul(ps_tail[:, cols], top2[:, n, cols], h1[:, n, :],
                                                  start=(n == 0), stop=(n == HID1 // P - 1))
                    mm.then_inc(s_h2_ps, 1)
                if u == 37:
                    pe.wait_ge(s_h2, t)
                    for n in range(HID2 // P):
                        mm = nc.tensor.matmul(ps_tail[0:1, 0:P], top3[:, n:n + 1], h2[:, n, :],
                                              start=(n == 0), stop=(n == HID2 // P - 1))
                    mm.then_inc(s_y_ps, 1)

            def tile(t, first=False, last=False):
                for u in range(TSLOTS):
                    c, k = u // SLOTS, u % SLOTS
                    up, fc, r = front_at(c, k)
                    front = not (last and up)
                    if u + 2 < TSLOTS:
                        spread_x0(t, (u + 2) // SLOTS, (u + 2) % SLOTS)
                    elif not last:
                        spread_x0(t + 1, 0, u + 2 - TSLOTS)
                    if front:
                        front_before(t + up, fc, r)
                    if u in (SPLIT_SLOT, SPLIT_SLOT + 1):
                        fields_of_units(t, u - SPLIT_SLOT)
                    layer2(t, c, k)
                    if front:
                        front_after(t + up, fc, r)
                    if not first:
                        tail(t, u)

            pe.wait_ge(s_consts, 4)
            for r in range(3):
                front_before(0, 0, r)
            pe.wait_ge(s_ws, 1)
            front_after(0, 0, 2)
            for r in range(3, 6):
                front_before(0, 0, r)
                front_after(0, 0, r)
            spread_x0(0, 0, 0)
            spread_x0(0, 0, 1)
            for r in range(3):
                front_before(0, 1, r)
            front_after(0, 1, 2)
            pe.wait_ge(s_wh, 1)
            pe.wait_ge(s_wl, 1)
            tile(0, first=True)
            pe.wait_ge(s_w2, LAND)
            pe.wait_ge(s_top, LAND * 6)
            with pe.Fori(1, TILES - 1) as t:
                tile(t)
            tile(TILES - 1, last=True)
            for u in range(TSLOTS):
                tail(TILES, u)

        @block.scalar
        def _(act):
            def front(t, c, r):
                g = CHUNKS * t + c
                if r == 1:
                    act.wait_ge(s_x0_ps, g + 1)
                    wait(act, s_spread, SLOTS * (g - CHUNKS + 1))
                    if c == 0:
                        wait(act, s_xn_ps, 2 * t)
                    nc.scalar.copy(x0t[:, c, :].rearrange("p (b i) -> p b i", i=DIM),
                                   ps_front[1][0:ROWS, :].rearrange("p (i b) -> p b i", i=DIM)
                                   ).then_inc(s_x0t, 1)
                if r == 2:
                    act.wait_ge(s_xa_ps, g + 1)
                    wait(act, s_z1, PAIRS * g)
                    nc.scalar.copy(xa[:, :], ps_front[0][0:ROWS, :]).then_inc(s_xa, 1)
                if r == 7:
                    act.wait_ge(s_l1, PAIRS * g + PAIRS)
                    wait(act, s_x1q, LAND * REPS * g)
                    wait(act, s_sums, g)
                    wait(act, s_z, SLOTS * (g - 1))
                    nc.scalar.copy(x1[:, :], ps_l1[:, :]).then_inc(s_x1, 1)

            def load_early(t):
                wait(act, s_emb_early, LAND * EARLY * t)
                act.dma_start(ids_early[:, :], ids_t[t, :, 0:EARLY]).then_inc(s_ids_early, LAND)

            def load_late(t):
                wait(act, s_emb_late, LAND * LATE * t)
                act.dma_start(ids_late[:, :], ids_t[t, :, EARLY:FIELDS]).then_inc(s_ids_late, LAND)

            def load_ctx(t):
                act.dma_start(ctxt[:, :], t_ctx[t]).then_inc(s_ctx, LAND)

            def split(t, step):
                if step == 0:
                    act.wait_ge(s_emb_early, LAND * EARLY * (t + 1))
                    act.wait_ge(s_emb_late, LAND * LATE * (t + 1))
                    wait(act, s_x0_ps, CHUNKS * t)
                    nc.scalar.copy(parts[:, :, 0:FIELDS],
                                   emb[:, :, :].rearrange("p f d -> p d f")).then_inc(s_hi, 1)
                else:
                    act.wait_ge(s_rest, t + 1)
                    nc.scalar.copy(parts[:, :, FIELDS:2 * FIELDS],
                                   emb[:, :, :].rearrange("p f d -> p d f")).then_inc(s_mid, 1)

            def round_z(t, u):
                j = TSLOTS * t + u
                act.wait_ge(s_z, j + 1)
                wait(act, s_l2, j - 1)
                p = parts_of(u % SLOTS)
                nc.scalar.copy(zh[0:p, u % 2, :], z[0:p, u % 2, :]).then_inc(s_zh, 1)

            def take_x2(t, c):
                g = CHUNKS * t + c
                act.wait_ge(s_l2, SLOTS * g + SLOTS)
                if c == 0:
                    wait(act, s_x2t_ps, UNITS // UG * t)
                nc.scalar.copy(x2[:, N * c:N * c + N], ps_l2[c % 2][:, :]).then_inc(s_x2, 1)

            def tail(t, u):
                if u == 5:
                    load_ctx(t - 1)
                if 3 <= u < 3 + UNITS // UG:
                    r = u - 3
                    act.wait_ge(s_x2t_ps, UNITS // UG * (t - 1) + r + 1)
                    nc.scalar.copy(x2t[:, UG * r:UG * r + UG, :],
                                   ps_tail[:, :].rearrange("p (i b) -> p i b", b=P)
                                   ).then_inc(s_x2t, 1)
                if 8 <= u < 8 + UNITS:
                    s = u - 8
                    act.wait_ge(s_gram_ps, UNITS * (t - 1) + s + 1)
                    nc.scalar.copy(gram[:, :, UB * s:UB * s + UB],
                                   ps_tail[:, 0:FC * UB].rearrange("p (f b) -> p f b", b=UB)
                                   ).then_inc(s_gram, 1)
                if u == 33:
                    act.wait_ge(s_l3, t)
                    nc.scalar.copy(sum3[:, :], ps_tail[:, 0:P]).then_inc(s_sum3, 1)
                if u == 35:
                    act.wait_ge(s_h1_ps, t)
                    for m in range(HID1 // P):
                        ins = nc.scalar.activation(h1[:, m, :], ps_tail[:, P * m:P * m + P],
                                                   ACT.Relu, bias=b1[:, m:m + 1])
                    ins.then_inc(s_h1, 1)
                if u == 37:
                    act.wait_ge(s_h2_ps, t)
                    for m in range(HID2 // P):
                        ins = nc.scalar.activation(h2[:, m, :], ps_tail[:, P * m:P * m + P],
                                                   ACT.Relu, bias=b2[:, m:m + 1])
                    ins.then_inc(s_h2, 1)
                if u == 39:
                    act.wait_ge(s_y_ps, t)
                    act.wait_ge(s_out, LAND * t)
                    nc.scalar.copy(y[:, :], ps_tail[0:1, 0:P]).then_inc(s_y, 1)
                    act.wait_ge(s_y, t)
                    act.dma_start(out_t[t - 1], y[:, :]).then_inc(s_out, LAND)

            def tile(t, first=False, last=False, gathers=True):
                for u in range(TSLOTS):
                    c, k = u // SLOTS, u % SLOTS
                    round_z(t, u)
                    if gathers and u == 0:
                        load_early(t + 2)
                    if gathers and u == GATHER_SLOT:
                        load_late(t + 2)
                    if k == 1 and u > 1:
                        take_x2(t, c - 1)
                    if u == 1 and not first:
                        take_x2(t - 1, CHUNKS - 1)
                    up, fc, r = front_at(c, k)
                    if not (last and up):
                        front(t + up, fc, r)
                    if not last and u in (SPLIT_SLOT, SPLIT_SLOT + 1):
                        split(t + 1, u - SPLIT_SLOT)
                    if u in (SPLIT_SLOT + 1, SPLIT_SLOT + 2):
                        half = u - SPLIT_SLOT - 1
                        act.wait_ge(s_xn_ps, 2 * t + half + 1)
                        wait(act, s_diag, UNITS * t)
                        nc.scalar.copy(xn[:, UNITS // 2 * half:UNITS // 2 * half + UNITS // 2, :],
                                       ps_front[0][:, 0:UNITS // 2 * FIELDS].rearrange(
                                           "p (s f) -> p s f", f=FIELDS)).then_inc(s_xn, 1)
                    if not first:
                        tail(t, u)

            act.nop().then_inc(s_out, LAND)
            act.wait_ge(s_sel, LAND * 3)
            at = 0
            for dst in (spread, pairsel):
                n = dst.shape[1] * dst.shape[2]
                nc.scalar.copy(dst[:, :, :].rearrange("p a b -> p (a b)"),
                               z_flat[0:ROWS, at:at + n]).then_inc(s_consts, 1)
                at += n
            nc.scalar.copy(joinsel[:, :], z_flat[0:ROWS, at:at + FIELDS]).then_inc(s_consts, 1)
            nc.scalar.copy(ident_bf[:, :], ident[:, :]).then_inc(s_consts, 1)
            act.wait_ge(s_w1, LAND)
            nc.scalar.copy(wh[:, :, :, :].rearrange("p a i b -> p (a i b)"),
                           gram[:, :, :].rearrange("p a b -> p (a b)")).then_inc(s_wh, 1)
            split(0, 0)
            split(0, 1)
            load_early(1)
            load_late(1)
            for r in range(8):
                front(0, 0, r)
            for r in range(3):
                front(0, 1, r)
            tile(0, first=True)
            with act.Fori(1, TILES - 2) as t:
                tile(t)
            tile(TILES - 2, gathers=False)
            tile(TILES - 1, last=True, gathers=False)
            take_x2(TILES - 1, CHUNKS - 1)
            for u in range(TSLOTS):
                tail(TILES, u)
            act.wait_ge(s_out, LAND * (TILES + 1))

        @block.vector
        def _(dve):
            def front(t, c, r):
                g = CHUNKS * t + c
                for i in {2: [0], 3: [1, 2], 4: [3, 4], 5: [5, 6]}.get(r, []):
                    dve.wait_ge(s_pair_ps, PAIRS * g + i + 1)
                    if i == 0:
                        dve.wait_ge(s_xa, g + 1)
                    wait(dve, s_l1, PAIRS * g + (i - RING + 1 if i >= RING else 0))
                    n = rows_of(i)
                    nc.vector.tensor_tensor(z1[0:n, i % RING, :], ps_front[(i + 1) % 2][0:n, :],
                                            xa[0:n, :], ALU.mult).then_inc(s_z1, 1)
                if r == 8:
                    dve.wait_ge(s_x1, g + 1)
                    if c == 0:
                        wait(dve, s_sum1, t)
                    nc.vector.tensor_reduce(sum1_next[:, CHUNK_B * c:CHUNK_B * c + CHUNK_B],
                                            x1[:, :].rearrange("p (b i) -> p b i", i=DIM),
                                            AX_X, ALU.add).then_inc(s_sums, 1)

            def split(t, step):
                if step == 0:
                    dve.wait_ge(s_hi, t + 1)
                    nc.vector.tensor_tensor(emb[:, :, :].rearrange("p f d -> p d f"),
                                            emb[:, :, :].rearrange("p f d -> p d f"),
                                            parts[:, :, 0:FIELDS], ALU.subtract
                                            ).then_inc(s_rest, 1)
                else:
                    dve.wait_ge(s_mid, t + 1)
                    dve.wait_ge(s_rest, t + 1)
                    nc.vector.tensor_tensor(parts[:, :, 2 * FIELDS:3 * FIELDS],
                                            emb[:, :, :].rearrange("p f d -> p d f"),
                                            parts[:, :, FIELDS:2 * FIELDS], ALU.subtract
                                            ).then_inc(s_parts, 1)

            def products(t, c, k):
                j = TSLOTS * t + SLOTS * c + k
                dve.wait_ge(s_spread, j + 1)
                if k == 0:
                    dve.wait_ge(s_x1q, LAND * REPS * (CHUNKS * t + c + 1))
                wait(dve, s_zh, j - 1)
                wait(dve, s_zl_pool, j - 1)
                wait(dve, s_zl_dve, j - 1)
                p = parts_of(k)
                nc.vector.tensor_tensor(z[0:p, k % 2, :].rearrange("p (i n) -> p i n", n=N),
                                        ps_spread[k % 2][0:p, None, :].broadcast_to([p, 4, N]),
                                        x1q[0:p, c % 2, :, :], ALU.mult).then_inc(s_z, 1)

            def rest(t, u):
                j = TSLOTS * t + u
                dve.wait_ge(s_zh, j + 1)
                wait(dve, s_l2, j - 1)
                p = parts_of(u % SLOTS)
                nc.vector.tensor_tensor(zl[0:p, u % 2, POOL_COLS:], z[0:p, u % 2, POOL_COLS:],
                                        zh[0:p, u % 2, POOL_COLS:].bitcast(F32),
                                        ALU.subtract).then_inc(s_zl_dve, 1)

            def move_sums(t):
                wait(dve, s_h1_ps, t)
                dve.wait_ge(s_sums, CHUNKS * t + CHUNKS)
                nc.vector.tensor_copy(sum1[:, :], sum1_next[:, :]).then_inc(s_sum1, 1)

            def tail(t, u):
                if 5 <= u < 5 + UNITS:
                    s = u - 5
                    dve.wait_ge(s_xn, 2 * t)
                    if s >= 2:
                        dve.wait_ge(s_gram_ps, UNITS * (t - 1) + s - 1)
                    nc.vector.tensor_tensor(
                        diag[:, s % 2, 0:FIELDS, :],
                        xn[:, s, :].rearrange("p (f o) -> p f o", o=1).broadcast_to([P, FIELDS, UB]),
                        mask[:, None, :].broadcast_to([P, FIELDS, UB]),
                        ALU.mult).then_inc(s_diag, 1)

            def tile(t, first=False, last=False):
                for u in range(TSLOTS):
                    c, k = u // SLOTS, u % SLOTS
                    if u + 1 < TSLOTS:
                        products(t, (u + 1) // SLOTS, (u + 1) % SLOTS)
                    elif not last:
                        products(t + 1, 0, 0)
                    rest(t, u)
                    if u == 35:
                        move_sums(t)
                    up, fc, r = front_at(c, k)
                    if not (last and up):
                        front(t + up, fc, r)
                    if not last and u in (SPLIT_SLOT, SPLIT_SLOT + 1):
                        split(t + 1, u - SPLIT_SLOT)
                    if not first:
                        tail(t, u)

            dve.wait_ge(s_sel, LAND * 3)
            for h in range(2):
                nc.vector.tensor_copy(diag[:, h, FIELDS, :], mask[:, :])
            dve.wait_ge(s_w0, LAND * 2)
            nc.vector.tensor_tensor(ws[:, :, :].rearrange("p i m -> p (i m)"),
                                    ws[:, :, :].rearrange("p i m -> p (i m)"),
                                    x2[0:ROWS, 0:PAIRS * P], ALU.add).then_inc(s_ws, 1)
            dve.wait_ge(s_wh, 1)
            nc.vector.tensor_tensor(wl[:, :, :, :].rearrange("p a i b -> p (a i b)"),
                                    gram[:, :, :].rearrange("p a b -> p (a b)"),
                                    wh[:, :, :, :].rearrange("p a i b -> p (a i b)").bitcast(F32),
                                    ALU.subtract).then_inc(s_wl, 1)
            split(0, 0)
            split(0, 1)
            for r in range(9):
                front(0, 0, r)
            for r in range(3):
                front(0, 1, r)
            dve.wait_ge(s_consts, 4)
            products(0, 0, 0)
            tile(0, first=True)
            with dve.Fori(1, TILES - 1) as t:
                tile(t)
            tile(TILES - 1, last=True)
            for u in range(TSLOTS):
                tail(TILES, u)


def kernel(**inputs):
    import numpy as np
    import concourse.bacc as bacc
    from concourse.bass_utils import run_bass_kernel_spmd as run

    nc = bacc.Bacc("TRN2", target_bir_lowering=False, num_devices=1,
                   dynamic_dma_scratch_size=8192)

    def selectors():
        out = np.zeros((3, FIELDS, SLOTS * P + (1 + PAIRS) * ROWS + FIELDS), np.float32)
        for k in range(SLOTS):
            for q in range(QUADS):
                if QUADS * k + q < FIELDS:
                    at = P * k + QP * q
                    out[:, QUADS * k + q, at:at + QP] = 1
        for f in range(FIELDS):
            for n in range(DELTAS):
                out[:, f, SLOTS * P + FIELDS * n + f] = 1
                for i in range(PAIRS):
                    at = SLOTS * P + (1 + i) * ROWS + FIELDS * n
                    out[:, (f + DELTAS * i + n) % FIELDS, at + f] = 1
            out[:, f, SLOTS * P + (1 + PAIRS) * ROWS + f] = 1
        return out.reshape(ROWS, -1)

    def pair_rows(w):
        w = w.reshape(FIELDS, FIELDS, P)
        f = np.arange(FIELDS)
        upper, lower = (np.zeros((PAIRS * DELTAS, FIELDS, P), w.dtype) for _ in range(2))
        for delta in range(20):
            g = (f + delta) % FIELDS
            upper[delta] = w[f, g]
            if delta:
                lower[delta] = w[g, f]
        return [x.reshape(PAIRS, ROWS, P).transpose(1, 0, 2) for x in (upper, lower)]

    def slot_rows(w):
        full = np.zeros((SLOTS * QUADS, P, P), w.dtype)
        full[:FIELDS] = w.reshape(FIELDS, P, P)
        full = full.reshape(SLOTS, QUADS, 4, QP, P).transpose(1, 3, 0, 2, 4)
        return full.reshape(P, SLOTS * 4, P)

    upper, lower = pair_rows(np.asarray(inputs["L0_rec_f0"]))
    arrays = {
        "ids": np.asarray(inputs["ids"]),
        "ctxt": np.asarray(inputs["dense_ctx"]).reshape(TILES, P, CTX).transpose(0, 2, 1),
        "wu": upper, "wl": lower,
        "w1": slot_rows(np.asarray(inputs["L0_rec_f1"])),
        "w2": np.asarray(inputs["L0_rec_f2"]).reshape(FIELDS, P, P).transpose(1, 0, 2),
        "top1": np.asarray(inputs["W_top1"]),
        "b1": np.asarray(inputs["b_top1"]).reshape(HID1 // P, P).T,
        "top2": np.asarray(inputs["W_top2"]),
        "b2": np.asarray(inputs["b_top2"]).reshape(HID2 // P, P).T,
        "top3": np.asarray(inputs["W_top3"]).reshape(HID2 // P, P).T,
        "sel": selectors(),
        "ident": np.eye(P, dtype=np.float32),
        "mask": np.repeat(np.eye(UB, dtype=np.float32), DIM, axis=0),
    }
    for f in range(FIELDS):
        arrays[f"tbl_{f}"] = np.asarray(inputs[f"tbl_{f}"])
    arrays = {f"in_{k}": np.ascontiguousarray(a) for k, a in arrays.items()}
    ap = {k[3:]: nc.dram_tensor(k, a.shape, mybir.dt.from_np(a.dtype), kind="ExternalInput").ap()
          for k, a in arrays.items()}
    out = nc.dram_tensor("out", (BATCH, 1), F32, kind="ExternalOutput").ap()
    build(nc, ap["ids"], [ap[f"tbl_{f}"] for f in range(FIELDS)], ap["ctxt"], ap["wu"], ap["wl"],
          ap["w1"], ap["w2"], ap["top1"], ap["b1"], ap["top2"], ap["b2"], ap["top3"], ap["sel"],
          ap["ident"], ap["mask"], out)
    return run(nc, [arrays], core_ids=[0]).results[0]["out"]
```

```python
from contextlib import ExitStack

import concourse.bass as bass
from concourse import mybir

F32 = mybir.dt.float32
F32R = mybir.dt.float32r
I32 = mybir.dt.int32
U32 = mybir.dt.uint32
ALU = mybir.AluOpType
ACT = mybir.ActivationFunctionType
AX_X = mybir.AxisListType.X

P = 128
FIELDS = 39
DIM = 16
BATCH = 1024
TILES = BATCH // P
CHUNK_B = 32
CHUNKS = P // CHUNK_B
N = CHUNK_B * DIM
QUADS = 4
QP = P // QUADS
SLOTS = -(-FIELDS // QUADS)
TSLOTS = CHUNKS * SLOTS
LAST_P = (FIELDS - QUADS * (SLOTS - 1)) * QP
DELTAS = 3
ROWS = DELTAS * FIELDS
PAIRS = 7
LAST_ROWS = (20 - DELTAS * (PAIRS - 1)) * FIELDS
WRAP = 19
RING = 4
SHIFTS = 3
SPREADS = 4
UB = 8
UNITS = CHUNK_B // UB
FC = FIELDS + 1
HID1, HID2, CTX = 512, 256, 16
POOL_COLS = 1120
FRONT = 3
STAGE_SLOT = 20
L3_SLOT, L3_SLOTS = 8, 6
H1_SLOT = 17
H2_SLOT = 24
Y_SLOT = 29
GATHER_SLOT = 22
LATE = 19
EARLY = FIELDS - LATE
LAND = 16


def build(nc, t_ids, t_tables, t_ctx, t_wu, t_wl, t_w1, t_w2, t_top1, t_b1, t_top2, t_b2, t_top3,
          t_ident, t_mask, x0_dram, x1_dram, t_out):
    with ExitStack() as ctx:
        def sb(name, shape, dt=F32):
            return ctx.enter_context(nc.sbuf_tensor(name, shape, dt))

        def bank(name):
            return ctx.enter_context(nc.psum_tensor(name, [P, 512], F32))

        def sem(name):
            return ctx.enter_context(nc.semaphore(name))

        ident = sb("ident", [P, P])
        mask = sb("mask", [P, UB])
        ws = sb("ws", [ROWS, PAIRS, P])
        wh = sb("wh", [P, SLOTS, 4, P], F32R)
        wl = sb("wl", [P, SLOTS, 4, P], F32R)
        w2 = sb("w2", [P, FIELDS, P])
        top1 = sb("top1", [P, 3, HID1])
        top1c = sb("top1c", [CTX, HID1])
        top2 = sb("top2", [P, HID1 // P, HID2])
        top3 = sb("top3", [P, HID2 // P])
        b1 = sb("b1", [P, HID1 // P])
        b2 = sb("b2", [P, HID2 // P])
        ids_early = sb("ids_early", [P, EARLY], I32)
        ids_late = sb("ids_late", [P, LATE], I32)
        emb = sb("emb", [P, FIELDS, DIM])
        staged = sb("staged", [P, FIELDS, DIM])
        x0_spread = sb("x0_spread", [P, SPREADS, N])
        x0_fields = sb("x0_fields", [FIELDS, N])
        x0_same = sb("x0_same", [ROWS, N])
        x0_shift = sb("x0_shift", [ROWS, SHIFTS, N])
        z1 = sb("z1", [ROWS, RING, N])
        x1 = sb("x1", [P, N])
        x1q = sb("x1q", [P, 2, 4, N])
        w0_lower = x1q[0:ROWS, 0, :, :].rearrange("p j n -> p (j n)")[:, 0:PAIRS * P]
        z = sb("z", [P, 2, 4 * N])
        zh = sb("zh", [P, 2, 4 * N], F32R)
        zl = sb("zl", [P, 2, 4 * N], F32R)
        x2 = sb("x2", [P, N])
        x2t = sb("x2t", [P, UNITS, P])
        diag = sb("diag", [P, UNITS, FC, UB])
        gram = sb("gram", [P, FC, P])
        sum1_next = sb("sum1_next", [P, P])
        sum1 = sb("sum1", [P, P])
        sum2 = sb("sum2", [P, P])
        sum3 = sb("sum3", [P, P])
        ctxt = sb("ctxt", [CTX, P])
        h1 = sb("h1", [P, HID1 // P, P])
        h2 = sb("h2", [P, HID2 // P, P])
        y = sb("y", [1, P])

        ps_l1 = bank("ps_l1")
        ps_l2 = [bank("ps_l2a"), bank("ps_l2b")]
        ps_turn = bank("ps_turn")
        ps_fields = bank("ps_fields")
        ps_gram = [bank("ps_gram0"), bank("ps_gram1")]
        ps_mlp = bank("ps_mlp")

        s_masks = sem("s_masks")
        s_w0 = sem("s_w0")
        s_w1 = sem("s_w1")
        s_w2 = sem("s_w2")
        s_top = sem("s_top")
        s_ids_early = sem("s_ids_early")
        s_ids_late = sem("s_ids_late")
        s_ctx = sem("s_ctx")
        s_emb_early = sem("s_emb_early")
        s_emb_late = sem("s_emb_late")
        s_x0_dram = [sem("s_x0_dram0"), sem("s_x0_dram1")]
        s_same = sem("s_same")
        s_shift = [sem(f"s_shift{i}") for i in range(SHIFTS)]
        s_spread = [sem(f"s_spread{i}") for i in range(SPREADS)]
        s_fields = sem("s_fields")
        s_x1_dram = sem("s_x1_dram")
        s_x1q = sem("s_x1q")
        s_out = sem("s_out")
        s_wh = sem("s_wh")
        s_ws = sem("s_ws")
        s_wl = sem("s_wl")
        s_staged = sem("s_staged")
        s_z1 = sem("s_z1")
        s_l1 = sem("s_l1")
        s_x1 = sem("s_x1")
        s_sums = sem("s_sums")
        s_sum1 = sem("s_sum1")
        s_z = sem("s_z")
        s_zh = sem("s_zh")
        s_zl_dve = sem("s_zl_dve")
        s_zl_pool = sem("s_zl_pool")
        s_l2 = sem("s_l2")
        s_x2 = sem("s_x2")
        s_xn = sem("s_xn")
        s_x2t_ps = sem("s_x2t_ps")
        s_x2t = sem("s_x2t")
        s_diag = sem("s_diag")
        s_ones = sem("s_ones")
        s_gram_ps = sem("s_gram_ps")
        s_gram = sem("s_gram")
        s_sum2 = sem("s_sum2")
        s_l3 = sem("s_l3")
        s_sum3 = sem("s_sum3")
        s_h1_ps = sem("s_h1_ps")
        s_h1 = sem("s_h1")
        s_h2_ps = sem("s_h2_ps")
        s_h2 = sem("s_h2")
        s_y_ps = sem("s_y_ps")
        s_y = sem("s_y")

        block = ctx.enter_context(nc.Block())

        def wait(eng, s, count):
            if isinstance(count, int) and count <= 0:
                return
            eng.wait_ge(s, count)

        def front_at(t, c, k, last):
            work = []
            for ahead, step in ((1, k + SLOTS - FRONT), (2, k - FRONT)):
                if step >= 0 and not (last and c + ahead >= CHUNKS):
                    work.append((t + (c + ahead) // CHUNKS, (c + ahead) % CHUNKS, step))
            return work

        def before(t, c):
            return (t, c - 1) if c else (t - 1, CHUNKS - 1)

        def rows_of(i):
            return LAST_ROWS if i == PAIRS - 1 else ROWS

        def parts_of(k):
            return LAST_P if k == SLOTS - 1 else P

        def stores_of(t, c):
            return LAND * 2 * (CHUNKS // 2 * t + c // 2 + 1)

        def shifts_of(t, c, i):
            per_chunk = -(-(PAIRS - i % SHIFTS) // SHIFTS)
            return LAND * (per_chunk * (CHUNKS * t + c) + i // SHIFTS + 1)

        ids_t = t_ids.rearrange("(t p) f -> t p f", p=P)
        out_t = t_out.rearrange("(t p) o -> t o p", p=P)

        @block.sync
        def _(sp):
            def load_spread(t, u):
                wait(sp, s_z, TSLOTS * t + u - SPREADS + 1)
                c, k = u // SLOTS, u % SLOTS
                p = parts_of(k)
                sp.dma_start(x0_spread[0:p, u % SPREADS, :],
                             x0_dram[c, QUADS * k:QUADS * k + p // QP, None, :].broadcast_to(
                                 [p // QP, QP, N])).then_inc(s_spread[u % SPREADS], LAND)

            def load_fields(t, c):
                wait(sp, s_xn, CHUNKS * t + c)
                sp.dma_start(x0_fields[:, :], x0_dram[c, 0:FIELDS, :]).then_inc(s_fields, LAND)

            def front(t, c, r):
                g = CHUNKS * t + c
                if r == 1:
                    sp.wait_ge(s_x0_dram[c % 2], stores_of(t, c))
                    if isinstance(t, int) and g == 1:
                        sp.wait_ge(s_z1, PAIRS)
                    rows = x0_dram[c, None, 0:FIELDS, :].broadcast_to([DELTAS, FIELDS, N])
                    sp.dma_start(x0_same[:, :], rows).then_inc(s_same, LAND)
                if 1 <= r < 1 + PAIRS:
                    i = r - 1
                    if i >= SHIFTS:
                        sp.wait_ge(s_z1, PAIRS * g + i - SHIFTS + 1)
                    n = rows_of(i)
                    first = x0_dram[c, DELTAS * i, 0:1]
                    rows = bass.AP(first.tensor, first.offset, [[N, n // FIELDS], [N, FIELDS], [1, N]])
                    sp.dma_start(x0_shift[0:n, i % SHIFTS, :], rows).then_inc(
                        s_shift[i % SHIFTS], LAND)
                if r == 12:
                    sp.wait_ge(s_x1, g + 1)
                    sp.dma_start(x1_dram.rearrange("i (j n) -> j i n", j=4), x1[:, :]
                                 ).then_inc(s_x1_dram, LAND)
                if r == 13:
                    sp.wait_ge(s_x1_dram, LAND * (g + 1))
                    sp.dma_start(x1q[:, c % 2, :, :].rearrange("p j n -> p (j n)"),
                                 x1_dram[None, :, :].broadcast_to([QUADS, QP, 4 * N])
                                 ).then_inc(s_x1q, LAND)

            def tile(t, first=False, last=False):
                for u in range(TSLOTS):
                    c, k = u // SLOTS, u % SLOTS
                    ahead = u + SPREADS - 1
                    if ahead < TSLOTS:
                        load_spread(t, ahead)
                    elif not last:
                        load_spread(t + 1, ahead - TSLOTS)
                    if k == 0 and not (first and c == 0):
                        load_fields(*before(t, c))
                    for work in front_at(t, c, k, last):
                        front(*work)

            sp.dma_start(ids_early[:, :], ids_t[0, :, 0:EARLY]).then_inc(s_ids_early, LAND)
            sp.dma_start(ids_late[:, :], ids_t[0, :, EARLY:FIELDS]).then_inc(s_ids_late, LAND)
            sp.dma_start(mask[:, :], t_mask).then_inc(s_masks, LAND)
            sp.dma_start(ident[:, :], t_ident).then_inc(s_masks, LAND)
            sp.dma_start(ws[:, :, :], t_wu).then_inc(s_w0, LAND)
            sp.dma_start(w0_lower, t_wl.rearrange("p i m -> p (i m)")).then_inc(s_w0, LAND)
            sp.dma_start(gram[:, :, :], t_w1[:, 0:SLOTS * 4, :]).then_inc(s_w1, LAND)
            sp.dma_start(w2[:, :, :], t_w2).then_inc(s_w2, LAND)
            for dst, src in ((top1[:, :, :], t_top1[0:3 * P, :].rearrange("(k p) n -> p k n", p=P)),
                             (top1c[:, :], t_top1[3 * P:3 * P + CTX, :]),
                             (top2[:, :, :], t_top2.rearrange("(k p) n -> p k n", p=P)),
                             (top3[:, :], t_top3), (b1[:, :], t_b1), (b2[:, :], t_b2)):
                sp.dma_start(dst, src).then_inc(s_top, LAND)
            for r in range(1 + PAIRS):
                front(0, 0, r)
            for u in range(SPREADS - 1):
                load_spread(0, u)
            for r in range(1 + SHIFTS):
                front(0, 1, r)
            front(0, 0, 12)
            front(0, 0, 13)
            for r in range(1 + SHIFTS, SLOTS - FRONT):
                front(0, 1, r)
            tile(0, first=True)
            with sp.Fori(1, TILES - 1) as t:
                tile(t)
            tile(TILES - 1, last=True)
            load_fields(TILES - 1, CHUNKS - 1)

        @block.gpsimd
        def _(pool):
            def gather(t, f):
                ids, at, landed = ((ids_early, f, s_emb_early) if f < EARLY else
                                   (ids_late, f - EARLY, s_emb_late))
                pool.indirect_dma_start(
                    emb[:, f, :], None, t_tables[f],
                    bass.IndirectOffsetOnAxis(ap=ids[:, at:at + 1].bitcast(U32), axis=0),
                ).then_inc(landed, LAND)

            def may_gather(t, late):
                if late:
                    pool.wait_ge(s_ids_late, LAND * (t + 1))
                else:
                    pool.wait_ge(s_ids_early, LAND * (t + 1))
                    wait(pool, s_staged, t)

            def rest(t, u):
                j = TSLOTS * t + u
                pool.wait_ge(s_zh, j + 1)
                wait(pool, s_l2, j - 1)
                p = parts_of(u % SLOTS)
                nc.gpsimd.tensor_tensor(zl[0:p, u % 2, 0:POOL_COLS], z[0:p, u % 2, 0:POOL_COLS],
                                        zh[0:p, u % 2, 0:POOL_COLS].bitcast(F32),
                                        ALU.subtract).then_inc(s_zl_pool, 1)

            def tile(t, near=True, far=True):
                for u in range(TSLOTS):
                    if near and u == 0:
                        may_gather(t + 1, late=True)
                    if far and u == GATHER_SLOT:
                        may_gather(t + 2, late=False)
                    rest(t, u)
                    if near and u < LATE:
                        gather(t + 1, EARLY + u)
                    if far and u >= GATHER_SLOT:
                        n = (u - GATHER_SLOT) * EARLY // (TSLOTS - GATHER_SLOT)
                        end = (u - GATHER_SLOT + 1) * EARLY // (TSLOTS - GATHER_SLOT)
                        for f in range(n, end):
                            gather(t + 2, f)

            may_gather(0, late=False)
            for f in range(EARLY):
                gather(0, f)
            may_gather(0, late=True)
            for f in range(EARLY, FIELDS):
                gather(0, f)
            may_gather(1, late=False)
            for f in range(EARLY):
                gather(1, f)
            tile(0)
            with pool.Fori(1, TILES - 2) as t:
                tile(t)
            tile(TILES - 2, far=False)
            tile(TILES - 1, near=False, far=False)

        @block.tensor
        def _(pe):
            def front(t, c, r):
                g = CHUNKS * t + c
                if 3 <= r < 3 + PAIRS:
                    i = r - 3
                    if i == 0:
                        wait(pe, s_x1, g)
                    pe.wait_ge(s_z1, PAIRS * g + i + 1)
                    n = rows_of(i)
                    nc.tensor.matmul(ps_l1[:, :], ws[0:n, i, :], z1[0:n, i % RING, :],
                                     start=(i == 0), stop=(i == PAIRS - 1)).then_inc(s_l1, 1)

            def fields_of_units(t, c):
                g = CHUNKS * t + c
                pe.wait_ge(s_fields, LAND * (g + 1))
                wait(pe, s_diag, g)
                for s in range(UNITS):
                    mm = nc.tensor.matmul(ps_fields[:, FIELDS * s:FIELDS * s + FIELDS],
                                          x0_fields[:, P * s:P * s + P],
                                          ident[0:FIELDS, 0:FIELDS], start=True, stop=True)
                mm.then_inc(s_xn, 1)

            def layer2(t, c, k):
                j = TSLOTS * t + SLOTS * c + k
                if k == 0:
                    wait(pe, s_x2, CHUNKS * t + c - 1)
                pe.wait_ge(s_zh, j + 1)
                pe.wait_ge(s_zl_dve, j + 1)
                pe.wait_ge(s_zl_pool, j + 1)
                p = parts_of(k)
                for i in range(4):
                    cols = slice(N * i, N * i + N)
                    for n, (w, x) in enumerate(((wh, zh), (wh, zl), (wl, zh))):
                        mm = nc.tensor.matmul(ps_l2[c % 2][:, :], w[0:p, k, i, :],
                                              x[0:p, k % 2, cols],
                                              start=(k == 0 and i == 0 and n == 0),
                                              stop=(k == SLOTS - 1 and i == 3 and n == 2))
                mm.then_inc(s_l2, 1)

            def unit_work(t, c, k):
                g = CHUNKS * t + c
                if k == 0:
                    pe.wait_ge(s_x2, g + 1)
                    wait(pe, s_x2t, g)
                    for s in range(UNITS):
                        mm = nc.tensor.transpose(ps_turn[:, P * s:P * s + P],
                                                 x2[:, P * s:P * s + P], ident[:, :])
                    mm.then_inc(s_x2t_ps, 1)
                if 3 <= k < 3 + UNITS:
                    s = k - 3
                    if s == 0:
                        pe.wait_ge(s_x2t, g + 1)
                        pe.wait_ge(s_diag, g + 1)
                    wait(pe, s_gram, UNITS * g + s - 1)
                    nc.tensor.matmul(ps_gram[s % 2][:, 0:FC * UB], x2t[:, s, :],
                                     diag[:, s, :, :].rearrange("p f b -> p (f b)"),
                                     start=True, stop=True).then_inc(s_gram_ps, 1)

            def tail(t, u):
                if L3_SLOT <= u < L3_SLOT + L3_SLOTS:
                    if u == L3_SLOT:
                        pe.wait_ge(s_gram, UNITS * CHUNKS * t)
                    n = u - L3_SLOT
                    for f in range(n * FIELDS // L3_SLOTS, (n + 1) * FIELDS // L3_SLOTS):
                        mm = nc.tensor.matmul(ps_mlp[:, 0:P], w2[:, f, :], gram[:, f, :],
                                              start=(f == 0), stop=(f == FIELDS - 1))
                    if n == L3_SLOTS - 1:
                        mm.then_inc(s_l3, 1)
                if H1_SLOT <= u < H1_SLOT + HID1 // P:
                    m = u - H1_SLOT
                    if m == 0:
                        pe.wait_ge(s_sum3, t)
                        pe.wait_ge(s_sum2, t)
                        pe.wait_ge(s_sum1, t)
                        pe.wait_ge(s_ctx, LAND * t)
                    cols = slice(P * m, P * m + P)
                    for n, (w, x) in enumerate(((top1[:, 0, cols], sum1[:, :]),
                                                (top1[:, 1, cols], sum2[:, :]),
                                                (top1[:, 2, cols], sum3[:, :]),
                                                (top1c[:, cols], ctxt[:, :]))):
                        mm = nc.tensor.matmul(ps_mlp[:, cols], w, x, start=(n == 0), stop=(n == 3))
                    if m == HID1 // P - 1:
                        mm.then_inc(s_h1_ps, 1)
                if H2_SLOT <= u < H2_SLOT + HID2 // P:
                    m = u - H2_SLOT
                    if m == 0:
                        pe.wait_ge(s_h1, t)
                    cols = slice(P * m, P * m + P)
                    for n in range(HID1 // P):
                        mm = nc.tensor.matmul(ps_mlp[:, cols], top2[:, n, cols], h1[:, n, :],
                                              start=(n == 0), stop=(n == HID1 // P - 1))
                    if m == HID2 // P - 1:
                        mm.then_inc(s_h2_ps, 1)
                if u == Y_SLOT:
                    pe.wait_ge(s_h2, t)
                    for n in range(HID2 // P):
                        mm = nc.tensor.matmul(ps_mlp[0:1, 0:P], top3[:, n:n + 1], h2[:, n, :],
                                              start=(n == 0), stop=(n == HID2 // P - 1))
                    mm.then_inc(s_y_ps, 1)

            def tile(t, first=False, last=False):
                for u in range(TSLOTS):
                    c, k = u // SLOTS, u % SLOTS
                    if k == 2 and not (first and c == 0):
                        fields_of_units(*before(t, c))
                    layer2(t, c, k)
                    for work in front_at(t, c, k, last):
                        front(*work)
                    if not (first and c == 0):
                        unit_work(*before(t, c), k)
                    if not first:
                        tail(t, u)

            pe.wait_ge(s_ws, 1)
            for r in range(3 + PAIRS):
                front(0, 0, r)
            for r in range(SLOTS - FRONT):
                front(0, 1, r)
            pe.wait_ge(s_wh, 1)
            pe.wait_ge(s_wl, 1)
            pe.wait_ge(s_masks, LAND * 2)
            tile(0, first=True)
            pe.wait_ge(s_w2, LAND)
            pe.wait_ge(s_top, LAND * 6)
            with pe.Fori(1, TILES - 1) as t:
                tile(t)
            tile(TILES - 1, last=True)
            fields_of_units(TILES - 1, CHUNKS - 1)
            for k in range(SLOTS):
                unit_work(TILES - 1, CHUNKS - 1, k)
            for u in range(TSLOTS):
                tail(TILES, u)

        @block.scalar
        def _(act):
            def front(t, c, r):
                g = CHUNKS * t + c
                if r == 0:
                    act.wait_ge(s_staged, t + 1)
                    if not (isinstance(t, int) and g == 1):
                        wait(act, s_z1, PAIRS * g)
                    src = staged[CHUNK_B * c:CHUNK_B * c + CHUNK_B, :, :]
                    dst = x0_dram[c].rearrange("f (b i) -> b f i", i=DIM)
                    for at, n in ((0, FIELDS), (FIELDS, WRAP)):
                        act.dma_start(dst[:, at:at + n, :], src[:, 0:n, :]
                                      ).then_inc(s_x0_dram[c % 2], LAND)
                if r == 11:
                    act.wait_ge(s_l1, PAIRS * g + PAIRS)
                    wait(act, s_x1q, LAND * g)
                    wait(act, s_sums, g)
                    wait(act, s_z, SLOTS * (g - 1))
                    nc.scalar.copy(x1[:, :], ps_l1[:, :]).then_inc(s_x1, 1)

            def load_early(t):
                wait(act, s_emb_early, LAND * EARLY * t)
                act.dma_start(ids_early[:, :], ids_t[t, :, 0:EARLY]).then_inc(s_ids_early, LAND)

            def load_late(t):
                wait(act, s_emb_late, LAND * LATE * t)
                act.dma_start(ids_late[:, :], ids_t[t, :, EARLY:FIELDS]).then_inc(s_ids_late, LAND)

            def load_ctx(t):
                act.dma_start(ctxt[:, :], t_ctx[t]).then_inc(s_ctx, LAND)

            def stage(t):
                act.wait_ge(s_emb_early, LAND * EARLY * (t + 1))
                act.wait_ge(s_emb_late, LAND * LATE * (t + 1))
                for c in (2, 3):
                    wait(act, s_x0_dram[c % 2], stores_of(t - 1, c))
                nc.scalar.copy(staged[:, :, :].rearrange("p f i -> p (f i)"),
                               emb[:, :, :].rearrange("p f i -> p (f i)")).then_inc(s_staged, 1)

            def round_z(t, u):
                j = TSLOTS * t + u
                act.wait_ge(s_z, j + 1)
                wait(act, s_l2, j - 1)
                p = parts_of(u % SLOTS)
                nc.scalar.copy(zh[0:p, u % 2, :], z[0:p, u % 2, :]).then_inc(s_zh, 1)

            def take_x2(t, c):
                g = CHUNKS * t + c
                act.wait_ge(s_l2, SLOTS * g + SLOTS)
                wait(act, s_x2t_ps, g)
                nc.scalar.copy(x2[:, :], ps_l2[c % 2][:, :]).then_inc(s_x2, 1)

            def unit_work(t, c, k):
                g = CHUNKS * t + c
                if k == 3:
                    act.wait_ge(s_xn, g + 1)
                    for b in range(UB):
                        ins = nc.scalar.mul(diag[:, :, 0:FIELDS, b],
                                            ps_fields[:, 0:UNITS * FIELDS].rearrange(
                                                "p (s f) -> p s f", f=FIELDS), mask[:, b:b + 1])
                    ins.then_inc(s_diag, 1)
                if k == 2:
                    act.wait_ge(s_x2t_ps, g + 1)
                    nc.scalar.copy(x2t[:, :, :].rearrange("p s g -> p (s g)"),
                                   ps_turn[:, :]).then_inc(s_x2t, 1)

            def take_gram(t, c, s):
                act.wait_ge(s_gram_ps, UNITS * (CHUNKS * t + c) + s + 1)
                if c == 0 and s == 0:
                    wait(act, s_l3, t)
                    wait(act, s_sum2, t)
                at = CHUNK_B * c + UB * s
                nc.scalar.copy(gram[:, :, at:at + UB],
                               ps_gram[s % 2][:, 0:FC * UB].rearrange("p (f b) -> p f b", b=UB)
                               ).then_inc(s_gram, 1)

            def tail(t, u):
                if u == 5:
                    load_ctx(t - 1)
                if u == 9:
                    act.wait_ge(s_gram, UNITS * CHUNKS * t)
                    nc.scalar.copy(sum2[:, :], gram[:, FIELDS, :]).then_inc(s_sum2, 1)
                if u == L3_SLOT + L3_SLOTS + 1:
                    act.wait_ge(s_l3, t)
                    nc.scalar.copy(sum3[:, :], ps_mlp[:, 0:P]).then_inc(s_sum3, 1)
                if u == H1_SLOT + HID1 // P + 1:
                    act.wait_ge(s_h1_ps, t)
                    for m in range(HID1 // P):
                        ins = nc.scalar.activation(h1[:, m, :], ps_mlp[:, P * m:P * m + P],
                                                   ACT.Relu, bias=b1[:, m:m + 1])
                    ins.then_inc(s_h1, 1)
                if u == H2_SLOT + HID2 // P + 1:
                    act.wait_ge(s_h2_ps, t)
                    for m in range(HID2 // P):
                        ins = nc.scalar.activation(h2[:, m, :], ps_mlp[:, P * m:P * m + P],
                                                   ACT.Relu, bias=b2[:, m:m + 1])
                    ins.then_inc(s_h2, 1)
                if u == Y_SLOT + 2:
                    act.wait_ge(s_y_ps, t)
                    act.wait_ge(s_out, LAND * t)
                    nc.scalar.copy(y[:, :], ps_mlp[0:1, 0:P]).then_inc(s_y, 1)
                    act.wait_ge(s_y, t)
                    act.dma_start(out_t[t - 1], y[:, :]).then_inc(s_out, LAND)

            def tile(t, first=False, last=False, gathers=True):
                for u in range(TSLOTS):
                    c, k = u // SLOTS, u % SLOTS
                    round_z(t, u)
                    if gathers and u == 0:
                        load_early(t + 2)
                    if gathers and u == GATHER_SLOT:
                        load_late(t + 2)
                    if k == 1 and u > 1:
                        take_x2(t, c - 1)
                    if u == 1 and not first:
                        take_x2(t - 1, CHUNKS - 1)
                    for work in front_at(t, c, k, last):
                        front(*work)
                    if not last and u == STAGE_SLOT:
                        stage(t + 1)
                    if not (first and c == 0):
                        unit_work(*before(t, c), k)
                        if 5 <= k < 5 + UNITS:
                            take_gram(*before(t, c), k - 5)
                    if not first:
                        tail(t, u)

            act.nop().then_inc(s_out, LAND)
            act.wait_ge(s_masks, LAND * 2)
            act.wait_ge(s_ones, 1)
            act.wait_ge(s_w1, LAND)
            nc.scalar.copy(wh[:, :, :, :].rearrange("p a i b -> p (a i b)"),
                           gram[:, :, :].rearrange("p a b -> p (a b)")).then_inc(s_wh, 1)
            stage(0)
            front(0, 0, 0)
            front(0, 1, 0)
            load_early(1)
            load_late(1)
            front(0, 0, 11)
            tile(0, first=True)
            with act.Fori(1, TILES - 2) as t:
                tile(t)
            tile(TILES - 2, gathers=False)
            tile(TILES - 1, last=True, gathers=False)
            take_x2(TILES - 1, CHUNKS - 1)
            for k in range(SLOTS):
                unit_work(TILES - 1, CHUNKS - 1, k)
            for s in range(UNITS):
                take_gram(TILES - 1, CHUNKS - 1, s)
            for u in range(TSLOTS):
                tail(TILES, u)
            act.wait_ge(s_out, LAND * (TILES + 1))

        @block.vector
        def _(dve):
            def front(t, c, r):
                g = CHUNKS * t + c
                if 3 <= r < 3 + PAIRS:
                    i = r - 3
                    dve.wait_ge(s_shift[i % SHIFTS], shifts_of(t, c, i))
                    if i == 0:
                        dve.wait_ge(s_same, LAND * (g + 1))
                    wait(dve, s_l1, PAIRS * g + (i - RING + 1 if i >= RING else 0))
                    n = rows_of(i)
                    nc.vector.tensor_tensor(z1[0:n, i % RING, :], x0_shift[0:n, i % SHIFTS, :],
                                            x0_same[0:n, :], ALU.mult).then_inc(s_z1, 1)
                if r == 12:
                    dve.wait_ge(s_x1, g + 1)
                    if c == 0:
                        wait(dve, s_sum1, t)
                    nc.vector.tensor_reduce(sum1_next[:, CHUNK_B * c:CHUNK_B * c + CHUNK_B],
                                            x1[:, :].rearrange("p (b i) -> p b i", i=DIM),
                                            AX_X, ALU.add).then_inc(s_sums, 1)

            def products(t, c, k):
                u = SLOTS * c + k
                j = TSLOTS * t + u
                dve.wait_ge(s_spread[u % SPREADS],
                            LAND * (TSLOTS // SPREADS * t + u // SPREADS + 1))
                if k == 0:
                    dve.wait_ge(s_x1q, LAND * (CHUNKS * t + c + 1))
                wait(dve, s_zh, j - 1)
                wait(dve, s_zl_pool, j - 1)
                wait(dve, s_zl_dve, j - 1)
                p = parts_of(k)
                nc.vector.tensor_tensor(z[0:p, k % 2, :].rearrange("p (i n) -> p i n", n=N),
                                        x0_spread[0:p, u % SPREADS, None, :].broadcast_to([p, 4, N]),
                                        x1q[0:p, c % 2, :, :], ALU.mult).then_inc(s_z, 1)

            def rest(t, u):
                j = TSLOTS * t + u
                dve.wait_ge(s_zh, j + 1)
                wait(dve, s_l2, j - 1)
                p = parts_of(u % SLOTS)
                nc.vector.tensor_tensor(zl[0:p, u % 2, POOL_COLS:], z[0:p, u % 2, POOL_COLS:],
                                        zh[0:p, u % 2, POOL_COLS:].bitcast(F32),
                                        ALU.subtract).then_inc(s_zl_dve, 1)

            def move_sums(t):
                wait(dve, s_h1_ps, t)
                dve.wait_ge(s_sums, CHUNKS * t + CHUNKS)
                nc.vector.tensor_copy(sum1[:, :], sum1_next[:, :]).then_inc(s_sum1, 1)

            def tile(t, first=False, last=False):
                for u in range(TSLOTS):
                    c, k = u // SLOTS, u % SLOTS
                    if u + 1 < TSLOTS:
                        products(t, (u + 1) // SLOTS, (u + 1) % SLOTS)
                    elif not last:
                        products(t + 1, 0, 0)
                    rest(t, u)
                    if u == 35:
                        move_sums(t)
                    for work in front_at(t, c, k, last):
                        front(*work)

            dve.wait_ge(s_masks, LAND * 2)
            nc.vector.tensor_copy(diag[:, :, FIELDS, :],
                                  mask[:, None, :].broadcast_to([P, UNITS, UB])
                                  ).then_inc(s_ones, 1)
            dve.wait_ge(s_w0, LAND * 2)
            nc.vector.tensor_tensor(ws[:, :, :].rearrange("p i m -> p (i m)"),
                                    ws[:, :, :].rearrange("p i m -> p (i m)"),
                                    w0_lower, ALU.add).then_inc(s_ws, 1)
            dve.wait_ge(s_wh, 1)
            nc.vector.tensor_tensor(wl[:, :, :, :].rearrange("p a i b -> p (a i b)"),
                                    gram[:, :, :].rearrange("p a b -> p (a b)"),
                                    wh[:, :, :, :].rearrange("p a i b -> p (a i b)").bitcast(F32),
                                    ALU.subtract).then_inc(s_wl, 1)
            for r in range(13):
                front(0, 0, r)
            for r in range(SLOTS - FRONT):
                front(0, 1, r)
            products(0, 0, 0)
            tile(0, first=True)
            with dve.Fori(1, TILES - 1) as t:
                tile(t)
            tile(TILES - 1, last=True)


def kernel(**inputs):
    import numpy as np
    import concourse.bacc as bacc
    from concourse.bass_utils import run_bass_kernel_spmd as run

    nc = bacc.Bacc("TRN2", target_bir_lowering=False, num_devices=1,
                   dynamic_dma_scratch_size=8192)

    def pair_rows(w):
        w = w.reshape(FIELDS, FIELDS, P)
        f = np.arange(FIELDS)
        upper, lower = (np.zeros((PAIRS * DELTAS, FIELDS, P), w.dtype) for _ in range(2))
        for delta in range(20):
            g = (f + delta) % FIELDS
            upper[delta] = w[f, g]
            if delta:
                lower[delta] = w[g, f]
        return [x.reshape(PAIRS, ROWS, P).transpose(1, 0, 2) for x in (upper, lower)]

    def slot_rows(w):
        full = np.zeros((SLOTS * QUADS, P, P), w.dtype)
        full[:FIELDS] = w.reshape(FIELDS, P, P)
        full = full.reshape(SLOTS, QUADS, 4, QP, P).transpose(1, 3, 0, 2, 4)
        return full.reshape(P, SLOTS * 4, P)

    upper, lower = pair_rows(np.asarray(inputs["L0_rec_f0"]))
    arrays = {
        "ids": np.asarray(inputs["ids"]),
        "ctxt": np.asarray(inputs["dense_ctx"]).reshape(TILES, P, CTX).transpose(0, 2, 1),
        "wu": upper, "wl": lower,
        "w1": slot_rows(np.asarray(inputs["L0_rec_f1"])),
        "w2": np.asarray(inputs["L0_rec_f2"]).reshape(FIELDS, P, P).transpose(1, 0, 2),
        "top1": np.asarray(inputs["W_top1"]),
        "b1": np.asarray(inputs["b_top1"]).reshape(HID1 // P, P).T,
        "top2": np.asarray(inputs["W_top2"]),
        "b2": np.asarray(inputs["b_top2"]).reshape(HID2 // P, P).T,
        "top3": np.asarray(inputs["W_top3"]).reshape(HID2 // P, P).T,
        "ident": np.eye(P, dtype=np.float32),
        "mask": np.repeat(np.eye(UB, dtype=np.float32), DIM, axis=0),
    }
    for f in range(FIELDS):
        arrays[f"tbl_{f}"] = np.asarray(inputs[f"tbl_{f}"])
    arrays = {f"in_{k}": np.ascontiguousarray(a) for k, a in arrays.items()}
    ap = {k[3:]: nc.dram_tensor(k, a.shape, mybir.dt.from_np(a.dtype), kind="ExternalInput").ap()
          for k, a in arrays.items()}
    x0_dram = nc.dram_tensor("x0_dram", (CHUNKS, FIELDS + WRAP, N), F32, kind="Internal").ap()
    x1_dram = nc.dram_tensor("x1_dram", (QP, 4 * N), F32, kind="Internal").ap()
    out = nc.dram_tensor("out", (BATCH, 1), F32, kind="ExternalOutput").ap()
    build(nc, ap["ids"], [ap[f"tbl_{f}"] for f in range(FIELDS)], ap["ctxt"], ap["wu"], ap["wl"],
          ap["w1"], ap["w2"], ap["top1"], ap["b1"], ap["top2"], ap["b2"], ap["top3"], 
          ap["ident"], ap["mask"], x0_dram, x1_dram, out)
    return run(nc, [arrays], core_ids=[0]).results[0]["out"]
```

```python
from contextlib import ExitStack

import concourse.bass as bass
from concourse import mybir

F32 = mybir.dt.float32
F32R = mybir.dt.float32r
I32 = mybir.dt.int32
U32 = mybir.dt.uint32
ALU = mybir.AluOpType
ACT = mybir.ActivationFunctionType
AX_X = mybir.AxisListType.X

P = 128
FIELDS = 39
DIM = 16
BATCH = 1024
TILES = BATCH // P
CHUNK_B = 32
CHUNKS = P // CHUNK_B
N = CHUNK_B * DIM
QUADS = 4
QP = P // QUADS
SLOTS = -(-FIELDS // QUADS)
TSLOTS = CHUNKS * SLOTS
FIRST = FIELDS - QUADS * (SLOTS - 1)
SPREAD_BLOCKS = FIRST + SLOTS - 1
DELTAS = 3
ROWS = DELTAS * FIELDS
PAIRS = 7
WRAP = 20
PAIR_RING = 3
WARM_UP = 10
SPREADS = 4
HIGHS = 4
UB = 8
UNITS = CHUNK_B // UB
FC = FIELDS + 1
HID1, HID2, CTX = 512, 256, 16
FRONT = 3
STAGE_SLOT = 20
L3_SLOT = 7
L3_FIELDS = (4, 4, 4, 4, 4, 4, 7, 8)
H1_SLOTS = (18, 20, 25, 25)
H2_SLOTS = (29, 30)
Y_SLOT = 35
LOAD = 2
START = 6
IDS_SLOT = 4
GATHER_SLOT = 22
LATE = 19
EARLY = FIELDS - LATE
LAND = 16


def build(nc, t_ids, t_tables, t_ctx, t_wu, t_wl, t_w1, t_w2, t_top1, t_b1, t_top2, t_b2, t_top3,
          t_ident, t_mask, x0_dram, x1_dram, t_out):
    with ExitStack() as ctx:
        def sb(name, shape, dt=F32):
            return ctx.enter_context(nc.sbuf_tensor(name, shape, dt))

        def bank(name):
            return ctx.enter_context(nc.psum_tensor(name, [P, 512], F32))

        def sem(name):
            return ctx.enter_context(nc.semaphore(name))

        ident = sb("ident", [P, P])
        mask = sb("mask", [P, UB])
        ws = sb("ws", [ROWS, PAIRS, P])
        wh = sb("wh", [P, FIELDS, P], F32R)
        wl = sb("wl", [P, FIELDS, P], F32R)
        w2 = sb("w2", [P, FIELDS, P])
        top1 = sb("top1", [P, 3, HID1])
        top1c = sb("top1c", [CTX, HID1])
        top2 = sb("top2", [P, HID1 // P, HID2])
        top3 = sb("top3", [P, HID2 // P])
        b1 = sb("b1", [P, HID1 // P])
        b2 = sb("b2", [P, HID2 // P])
        ids_early = sb("ids_early", [P, EARLY], I32)
        ids_late = sb("ids_late", [P, LATE], I32)
        emb = sb("emb", [P, FIELDS, DIM])
        staged = sb("staged", [P, FIELDS, DIM])
        x0_spread = sb("x0_spread", [P, SPREADS, N])
        x0_fields = sb("x0_fields", [FIELDS, N])
        x0_same = sb("x0_same", [ROWS, N])
        pairs = sb("pairs", [ROWS, PAIR_RING, N])
        x1 = sb("x1", [P, N])
        x1q = sb("x1q", [P, 2, 4, N])
        w0_lower = x1q[0:ROWS, 0, :, :].rearrange("p j n -> p (j n)")[:, 0:PAIRS * P]
        z = sb("z", [P, 2, 4 * N])
        zh = sb("zh", [P, HIGHS, 4 * N], F32R)
        zl = sb("zl", [P, 2, 4 * N], F32R)
        x2 = sb("x2", [P, N])
        x2t = sb("x2t", [P, UNITS, P])
        diag = sb("diag", [P, UNITS, FC, UB])
        gram = sb("gram", [P, FC, P])
        sum1_next = sb("sum1_next", [P, P])
        sum1 = sb("sum1", [P, P])
        sum2 = sb("sum2", [P, P])
        sum3 = sb("sum3", [P, P])
        ctxt = sb("ctxt", [CTX, P])
        h1 = sb("h1", [P, HID1 // P, P])
        h2 = sb("h2", [P, HID2 // P, P])
        y = sb("y", [1, P])

        ps_l1 = bank("ps_l1")
        ps_l2 = [bank("ps_l2a"), bank("ps_l2b")]
        ps_turn = bank("ps_turn")
        ps_fields = bank("ps_fields")
        ps_gram = [bank("ps_gram0"), bank("ps_gram1")]
        ps_mlp = bank("ps_mlp")

        s_masks = sem("s_masks")
        s_w0 = sem("s_w0")
        s_w1 = sem("s_w1")
        s_w2 = sem("s_w2")
        s_top = sem("s_top")
        s_ids_early = sem("s_ids_early")
        s_ids_late = sem("s_ids_late")
        s_ctx = sem("s_ctx")
        s_emb_early = sem("s_emb_early")
        s_emb_late = sem("s_emb_late")
        s_x0_dram = [sem("s_x0_dram0"), sem("s_x0_dram1")]
        s_same = sem("s_same")
        s_shift = [sem(f"s_shift{i}") for i in range(PAIR_RING)]
        s_start = [sem(f"s_start{i}") for i in range(PAIRS - PAIR_RING)]
        s_spread = [sem(f"s_spread{i}") for i in range(SPREADS)]
        s_fields = sem("s_fields")
        s_x1_dram = sem("s_x1_dram")
        s_x1q = sem("s_x1q")
        s_out = sem("s_out")
        s_wh = sem("s_wh")
        s_ws = sem("s_ws")
        s_wl = sem("s_wl")
        s_staged = sem("s_staged")
        s_z1 = sem("s_z1")
        s_l1 = sem("s_l1")
        s_x1 = sem("s_x1")
        s_sums = sem("s_sums")
        s_sum1 = sem("s_sum1")
        s_z = sem("s_z")
        s_zh = sem("s_zh")
        s_zl_dve = sem("s_zl_dve")
        s_zl_pool = sem("s_zl_pool")
        s_l2 = sem("s_l2")
        s_x2 = sem("s_x2")
        s_xn = sem("s_xn")
        s_x2t_ps = sem("s_x2t_ps")
        s_x2t = sem("s_x2t")
        s_diag = sem("s_diag")
        s_ones = sem("s_ones")
        s_gram_ps = sem("s_gram_ps")
        s_gram = sem("s_gram")
        s_sum2 = sem("s_sum2")
        s_l3 = sem("s_l3")
        s_sum3 = sem("s_sum3")
        s_h1_ps = sem("s_h1_ps")
        s_h1 = sem("s_h1")
        s_h2_ps = sem("s_h2_ps")
        s_h2 = sem("s_h2")
        s_y_ps = sem("s_y_ps")
        s_y = sem("s_y")

        block = ctx.enter_context(nc.Block())

        def wait(eng, s, count):
            if isinstance(count, int) and count <= 0:
                return
            eng.wait_ge(s, count)

        def front_at(t, c, k, last):
            work = []
            for ahead, step in ((1, k + SLOTS - FRONT), (2, k - FRONT)):
                if step >= 0 and not (last and c + ahead >= CHUNKS):
                    work.append((t + (c + ahead) // CHUNKS, (c + ahead) % CHUNKS, step))
            return work

        def before(t, c):
            return (t, c - 1) if c else (t - 1, CHUNKS - 1)

        def blocks_of(k):
            return FIRST if k == 0 else 4

        def spread_wait(t, c, v):
            return LAND * (SPREAD_BLOCKS // SPREADS * (CHUNKS * t + c) + v // SPREADS + 1)

        def blocks_at(slots, u):
            return [m for m, slot in enumerate(slots) if slot == u]

        def gram_slots(c):
            return (5, 5, 6, 6) if c == 0 else (3, 3, 4, 4)

        def stores_of(t, c):
            return LAND * 2 * (CHUNKS // 2 * t + c // 2 + 1)

        def at_start(t, c, i):
            return isinstance(t, int) and (t, c) == (0, 0) and i >= PAIR_RING

        def pair_group(t, c, i):
            if at_start(t, c, i):
                return z[0:ROWS, 0, N * (i - PAIR_RING):N * (i - PAIR_RING) + N]
            return pairs[:, i % PAIR_RING, :]

        def pair_sem(t, c, i):
            if at_start(t, c, i):
                return s_start[i - PAIR_RING], LAND
            per_chunk = -(-(PAIRS - i % PAIR_RING) // PAIR_RING)
            count = per_chunk * (CHUNKS * t + c) + i // PAIR_RING + 1
            if not (isinstance(t, int) and (t, c) == (0, 0)):
                count = count - (per_chunk - 1)
            return s_shift[i % PAIR_RING], LAND * count

        def gathers_in(u):
            if u < GATHER_SLOT:
                return range(EARLY + u, EARLY + u + 1) if u < LATE else range(0)
            n, slots = u - GATHER_SLOT, TSLOTS - GATHER_SLOT
            return range(n * EARLY // slots, (n + 1) * EARLY // slots)

        def pool_cols(u, last):
            c, k = u // SLOTS, u % SLOTS
            gathers = 1 if last else len(gathers_in(u))
            pairs_here = [r for _, _, r in front_at(0, c, k, last) if 3 <= r < 3 + PAIRS]
            return 352 + 256 * blocks_of(k) - 320 * gathers + 192 * len(pairs_here)

        ids_t = t_ids.rearrange("(t p) f -> t p f", p=P)
        out_t = t_out.rearrange("(t p) o -> t o p", p=P)

        @block.sync
        def _(sp):
            def load_spread(t, c, v):
                f, n = (v, 1) if v < FIRST else (FIRST + QUADS * (v - FIRST), QUADS)
                sp.dma_start(x0_spread[:, v % SPREADS, :],
                             x0_dram[c, None, f:f + n, :].broadcast_to([P // n, n, N])
                             ).then_inc(s_spread[v % SPREADS], LAND)

            def load_spreads(t, c, k, last):
                wait(sp, s_z, TSLOTS * t + SLOTS * c + k)
                for v in (range(SPREADS, SPREADS + FIRST) if k == 1 else
                          (SPREADS - 1 if k == 0 else SPREADS + FIRST - 2 + k,)):
                    if v < SPREAD_BLOCKS:
                        load_spread(t, c, v)
                    elif not (last and c == CHUNKS - 1):
                        load_spread(t + (c + 1) // CHUNKS, (c + 1) % CHUNKS, v - SPREAD_BLOCKS)

            def load_fields(t, c):
                wait(sp, s_xn, CHUNKS * t + c)
                sp.dma_start(x0_fields[:, :], x0_dram[c, 0:FIELDS, :]).then_inc(s_fields, LAND)

            def front(t, c, r):
                g = CHUNKS * t + c
                if r == LOAD:
                    sp.wait_ge(s_x0_dram[c % 2], stores_of(t, c))
                    if isinstance(t, int) and g == 1:
                        sp.wait_ge(s_z1, PAIRS)
                    rows = x0_dram[c, 0:FIELDS, None, :].broadcast_to([FIELDS, DELTAS, N])
                    sp.dma_start(x0_same[:, :], rows).then_inc(s_same, LAND)
                if LOAD <= r < LOAD + PAIRS:
                    i = r - LOAD
                    held = i - PAIR_RING if i >= PAIR_RING else (
                        i + (PAIRS - 1 - i) // PAIR_RING * PAIR_RING - PAIRS)
                    if not at_start(t, c, i):
                        wait(sp, s_l1, PAIRS * g + held + 1)
                    first = x0_dram[c, DELTAS * i, 0:1]
                    rows = bass.AP(first.tensor, first.offset,
                                   [[N, FIELDS], [N, DELTAS], [1, N]])
                    sp.dma_start(pair_group(t, c, i), rows).then_inc(pair_sem(t, c, i)[0], LAND)
                if r == 12:
                    sp.wait_ge(s_x1, g + 1)
                    sp.dma_start(x1_dram, x1[:, :]).then_inc(s_x1_dram, LAND)
                if r == 13:
                    sp.wait_ge(s_x1_dram, LAND * (g + 1))
                    sp.dma_start(x1q[:, c % 2, :, :].rearrange("p j n -> p (j n)"),
                                 x1_dram.rearrange("(i j) n -> i (j n)", j=4)[:, None, :
                                                                             ].broadcast_to(
                                     [QP, QUADS, 4 * N])
                                 ).then_inc(s_x1q, LAND)

            def tile(t, first=False, last=False):
                for u in range(TSLOTS):
                    c, k = u // SLOTS, u % SLOTS
                    if not (first and u == 0):
                        load_spreads(t, c, k, last)
                    if k == 8:
                        load_fields(t, c)
                    for work in front_at(t, c, k, last):
                        front(*work)

            sp.dma_start(ids_early[:, :], ids_t[0, :, 0:EARLY]).then_inc(s_ids_early, LAND)
            sp.dma_start(ids_late[:, :], ids_t[0, :, EARLY:FIELDS]).then_inc(s_ids_late, LAND)
            sp.dma_start(mask[:, :], t_mask).then_inc(s_masks, LAND)
            sp.dma_start(ident[:, :], t_ident).then_inc(s_masks, LAND)
            sp.dma_start(ws[:, :, :], t_wu).then_inc(s_w0, LAND)
            sp.dma_start(w0_lower, t_wl.rearrange("p i m -> p (i m)")).then_inc(s_w0, LAND)
            sp.dma_start(gram[:, 0:FIELDS, :], t_w1).then_inc(s_w1, LAND)
            sp.dma_start(w2[:, :, :], t_w2).then_inc(s_w2, LAND)
            for dst, src in ((top1[:, :, :], t_top1[0:3 * P, :].rearrange("(k p) n -> p k n", p=P)),
                             (top1c[:, :], t_top1[3 * P:3 * P + CTX, :]),
                             (top2[:, :, :], t_top2.rearrange("(k p) n -> p k n", p=P)),
                             (top3[:, :], t_top3), (b1[:, :], t_b1), (b2[:, :], t_b2)):
                sp.dma_start(dst, src).then_inc(s_top, LAND)
            for r in range(LOAD + PAIRS):
                front(0, 0, r)
            for v in range(SPREADS):
                load_spread(0, 0, v)
            front(0, 0, 12)
            for r in range(LOAD, LOAD + PAIR_RING):
                front(0, 1, r)
            front(0, 0, 13)
            for r in range(LOAD + PAIR_RING, SLOTS - FRONT):
                front(0, 1, r)
            tile(0, first=True)
            with sp.Fori(1, TILES - 1) as t:
                tile(t)
            tile(TILES - 1, last=True)

        @block.gpsimd
        def _(pool):
            def gather(t, f):
                ids, at, landed = ((ids_early, f, s_emb_early) if f < EARLY else
                                   (ids_late, f - EARLY, s_emb_late))
                pool.indirect_dma_start(
                    emb[:, f, :], None, t_tables[f],
                    bass.IndirectOffsetOnAxis(ap=ids[:, at:at + 1].bitcast(U32), axis=0),
                ).then_inc(landed, LAND)

            def may_gather(t, late):
                if late:
                    pool.wait_ge(s_ids_late, LAND * (t + 1))
                else:
                    pool.wait_ge(s_ids_early, LAND * (t + 1))
                    wait(pool, s_staged, t)

            def rest(t, u, last):
                j = TSLOTS * t + u
                pool.wait_ge(s_zh, 2 * j + 1)
                wait(pool, s_l2, j - 1)
                n = pool_cols(u, last)
                nc.gpsimd.tensor_tensor(zl[:, u % 2, 0:n], z[:, u % 2, 0:n],
                                        zh[:, u % HIGHS, 0:n].bitcast(F32), ALU.subtract
                                        ).then_inc(s_zl_pool, 1)

            def tile(t, near=True, far=True):
                for u in range(TSLOTS):
                    if near and u == 0:
                        may_gather(t + 1, late=True)
                    if far and u == GATHER_SLOT:
                        may_gather(t + 2, late=False)
                    rest(t, u, last=not near)
                    if near and u < GATHER_SLOT:
                        for f in gathers_in(u):
                            gather(t + 1, f)
                    if far and u >= GATHER_SLOT:
                        for f in gathers_in(u):
                            gather(t + 2, f)

            may_gather(0, late=False)
            for f in range(EARLY):
                gather(0, f)
            may_gather(0, late=True)
            for f in range(EARLY, FIELDS):
                gather(0, f)
            may_gather(1, late=False)
            for f in range(EARLY):
                gather(1, f)
            tile(0)
            with pool.Fori(1, TILES - 2) as t:
                tile(t)
            tile(TILES - 2, far=False)
            tile(TILES - 1, near=False, far=False)

        @block.tensor
        def _(pe):
            def front(t, c, r):
                g = CHUNKS * t + c
                if 3 <= r < 3 + PAIRS:
                    i = r - 3
                    if i == 0:
                        wait(pe, s_x1, g)
                    pe.wait_ge(s_z1, PAIRS * g + i + 1)
                    nc.tensor.matmul(ps_l1[:, :], ws[:, i, :], pair_group(t, c, i),
                                     start=(i == 0), stop=(i == PAIRS - 1)).then_inc(s_l1, 1)

            def fields_of_units(t, c):
                g = CHUNKS * t + c
                pe.wait_ge(s_fields, LAND * (g + 1))
                wait(pe, s_diag, g)
                for s in range(UNITS):
                    mm = nc.tensor.matmul(ps_fields[:, FIELDS * s:FIELDS * s + FIELDS],
                                          x0_fields[:, P * s:P * s + P],
                                          ident[0:FIELDS, 0:FIELDS], start=True, stop=True)
                mm.then_inc(s_xn, 1)

            def layer2(t, c, k, last):
                u = SLOTS * c + k
                j = TSLOTS * t + u
                if k == 0:
                    wait(pe, s_x2, CHUNKS * t + c - 1)
                pool_blocks = pool_cols(u, last) // N
                for i in range(blocks_of(k)):
                    if i == 0:
                        pe.wait_ge(s_zh, 2 * j + 1)
                        pe.wait_ge(s_zl_pool, j + 1)
                    if i == pool_blocks:
                        pe.wait_ge(s_zh, 2 * j + 2)
                        pe.wait_ge(s_zl_dve, j + 1)
                    cols = slice(N * i, N * i + N)
                    at = i if k == 0 else FIRST + QUADS * (k - 1) + i
                    for n, (w, x) in enumerate(((wh, zh), (wh, zl), (wl, zh))):
                        mm = nc.tensor.matmul(ps_l2[c % 2][:, :], w[:, at, :],
                                              x[:, u % x.shape[1], cols],
                                              start=(k == 0 and i == 0 and n == 0),
                                              stop=(k == SLOTS - 1 and i == 3 and n == 2))
                mm.then_inc(s_l2, 1)

            def unit_work(t, c, k):
                g = CHUNKS * t + c
                if k == 0:
                    pe.wait_ge(s_x2, g + 1)
                    wait(pe, s_x2t, g)
                    for s in range(UNITS):
                        mm = nc.tensor.transpose(ps_turn[:, P * s:P * s + P],
                                                 x2[:, P * s:P * s + P], ident[:, :])
                    mm.then_inc(s_x2t_ps, 1)
                for s in blocks_at(gram_slots(c), k):
                    if s == 0:
                        pe.wait_ge(s_x2t, g + 1)
                        pe.wait_ge(s_diag, g + 1)
                    wait(pe, s_gram, UNITS * g + s - 1)
                    nc.tensor.matmul(ps_gram[s % 2][:, 0:FC * UB], x2t[:, s, :],
                                     diag[:, s, :, :].rearrange("p f b -> p (f b)"),
                                     start=True, stop=True).then_inc(s_gram_ps, 1)

            def tail(t, u):
                if L3_SLOT <= u < L3_SLOT + len(L3_FIELDS):
                    if u == L3_SLOT:
                        pe.wait_ge(s_gram, UNITS * CHUNKS * t)
                    n = u - L3_SLOT
                    for f in range(sum(L3_FIELDS[:n]), sum(L3_FIELDS[:n + 1])):
                        mm = nc.tensor.matmul(ps_mlp[:, 0:P], w2[:, f, :], gram[:, f, :],
                                              start=(f == 0), stop=(f == FIELDS - 1))
                    if n == len(L3_FIELDS) - 1:
                        mm.then_inc(s_l3, 1)
                for m in blocks_at(H1_SLOTS, u):
                    if m == 0:
                        pe.wait_ge(s_sum3, t)
                        pe.wait_ge(s_sum2, t)
                        pe.wait_ge(s_sum1, t)
                        pe.wait_ge(s_ctx, LAND * t)
                    cols = slice(P * m, P * m + P)
                    for n, (w, x) in enumerate(((top1[:, 0, cols], sum1[:, :]),
                                                (top1[:, 1, cols], sum2[:, :]),
                                                (top1[:, 2, cols], sum3[:, :]),
                                                (top1c[:, cols], ctxt[:, :]))):
                        mm = nc.tensor.matmul(ps_mlp[:, cols], w, x, start=(n == 0), stop=(n == 3))
                    if m == HID1 // P - 1:
                        mm.then_inc(s_h1_ps, 1)
                for m in blocks_at(H2_SLOTS, u):
                    if m == 0:
                        pe.wait_ge(s_h1, t)
                    cols = slice(P * m, P * m + P)
                    for n in range(HID1 // P):
                        mm = nc.tensor.matmul(ps_mlp[:, cols], top2[:, n, cols], h1[:, n, :],
                                              start=(n == 0), stop=(n == HID1 // P - 1))
                    if m == HID2 // P - 1:
                        mm.then_inc(s_h2_ps, 1)
                if u == Y_SLOT:
                    pe.wait_ge(s_h2, t)
                    for n in range(HID2 // P):
                        mm = nc.tensor.matmul(ps_mlp[0:1, 0:P], top3[:, n:n + 1], h2[:, n, :],
                                              start=(n == 0), stop=(n == HID2 // P - 1))
                    mm.then_inc(s_y_ps, 1)

            def tile(t, first=False, last=False):
                for u in range(TSLOTS):
                    c, k = u // SLOTS, u % SLOTS
                    if k == 0 and not (first and c == 0):
                        fields_of_units(*before(t, c))
                    if last and u == TSLOTS - 1:
                        fields_of_units(t, c)
                    layer2(t, c, k, last)
                    if first and u == 0:
                        for r in range(START, SLOTS - FRONT):
                            front(0, 1, r)
                    for work in front_at(t, c, k, last):
                        front(*work)
                    if not (first and c == 0):
                        unit_work(*before(t, c), k)
                    if not first:
                        tail(t, u)

            pe.wait_ge(s_masks, LAND * 2)
            pe.wait_ge(s_x0_dram[0], stores_of(0, 0))
            for _ in range(WARM_UP):
                nc.tensor.matmul(ps_mlp[:, 0:P], ident[:, :], ident[:, :], start=True, stop=True)
            pe.wait_ge(s_ws, 1)
            for r in range(3 + PAIRS):
                front(0, 0, r)
            for r in range(START):
                front(0, 1, r)
            pe.wait_ge(s_wh, 1)
            pe.wait_ge(s_wl, 1)
            tile(0, first=True)
            pe.wait_ge(s_w2, LAND)
            pe.wait_ge(s_top, LAND * 6)
            with pe.Fori(1, TILES - 1) as t:
                tile(t)
            tile(TILES - 1, last=True)
            for k in range(SLOTS):
                unit_work(TILES - 1, CHUNKS - 1, k)
            for u in range(TSLOTS):
                tail(TILES, u)

        @block.scalar
        def _(act):
            def front(t, c, r):
                g = CHUNKS * t + c
                if r == 0:
                    act.wait_ge(s_staged, t + 1)
                    if not (isinstance(t, int) and g == 1):
                        wait(act, s_z1, PAIRS * g)
                    src = staged[CHUNK_B * c:CHUNK_B * c + CHUNK_B, :, :]
                    dst = x0_dram[c].rearrange("f (b i) -> b f i", i=DIM)
                    for at, n in ((0, FIELDS), (FIELDS, WRAP)):
                        act.dma_start(dst[:, at:at + n, :], src[:, 0:n, :]
                                      ).then_inc(s_x0_dram[c % 2], LAND)
                if r == 11:
                    act.wait_ge(s_l1, PAIRS * g + PAIRS)
                    wait(act, s_x1q, LAND * g)
                    wait(act, s_sums, g)
                    wait(act, s_z, SLOTS * (g - 1) + 1)
                    nc.scalar.copy(x1[:, :], ps_l1[:, :]).then_inc(s_x1, 1)

            def load_early(t):
                wait(act, s_emb_early, LAND * EARLY * t)
                act.dma_start(ids_early[:, :], ids_t[t, :, 0:EARLY]).then_inc(s_ids_early, LAND)

            def load_late(t):
                wait(act, s_emb_late, LAND * LATE * t)
                act.dma_start(ids_late[:, :], ids_t[t, :, EARLY:FIELDS]).then_inc(s_ids_late, LAND)

            def load_ctx(t):
                act.dma_start(ctxt[:, :], t_ctx[t]).then_inc(s_ctx, LAND)

            def stage(t):
                act.wait_ge(s_emb_early, LAND * EARLY * (t + 1))
                act.wait_ge(s_emb_late, LAND * LATE * (t + 1))
                for c in (2, 3):
                    wait(act, s_x0_dram[c % 2], stores_of(t - 1, c))
                nc.scalar.copy(staged[:, :, :].rearrange("p f i -> p (f i)"),
                               emb[:, :, :].rearrange("p f i -> p (f i)")).then_inc(s_staged, 1)

            def round_z(t, u, last):
                j = TSLOTS * t + u
                act.wait_ge(s_z, j + 1)
                wait(act, s_l2, j - HIGHS + 1)
                n, end = pool_cols(u, last), N * blocks_of(u % SLOTS)
                nc.scalar.copy(zh[:, u % HIGHS, 0:n], z[:, u % 2, 0:n]).then_inc(s_zh, 1)
                nc.scalar.copy(zh[:, u % HIGHS, n:end], z[:, u % 2, n:end]).then_inc(s_zh, 1)

            def take_x2(t, c):
                g = CHUNKS * t + c
                act.wait_ge(s_l2, SLOTS * g + SLOTS)
                wait(act, s_x2t_ps, g)
                nc.scalar.copy(x2[:, :], ps_l2[c % 2][:, :]).then_inc(s_x2, 1)

            def spread_fields(t, c, rows):
                if rows[0] == 0:
                    act.wait_ge(s_xn, CHUNKS * t + c + 1)
                for b in rows:
                    ins = nc.scalar.mul(diag[:, :, 0:FIELDS, b],
                                        ps_fields[:, 0:UNITS * FIELDS].rearrange(
                                            "p (s f) -> p s f", f=FIELDS), mask[:, b:b + 1])
                if rows[-1] == UB - 1:
                    ins.then_inc(s_diag, 1)

            def turn_x2(t, c):
                act.wait_ge(s_x2t_ps, CHUNKS * t + c + 1)
                nc.scalar.copy(x2t[:, :, :].rearrange("p s g -> p (s g)"),
                               ps_turn[:, :]).then_inc(s_x2t, 1)

            def unit_work(t, c, k):
                if k == 3:
                    spread_fields(t, c, range(UB // 2, UB))
                if k == 2:
                    turn_x2(t, c)
                    spread_fields(t, c, range(UB // 2))

            def take_gram(t, c, s):
                act.wait_ge(s_gram_ps, UNITS * (CHUNKS * t + c) + s + 1)
                if c == 0 and s == 0:
                    wait(act, s_l3, t)
                    wait(act, s_sum2, t)
                at = CHUNK_B * c + UB * s
                nc.scalar.copy(gram[:, :, at:at + UB],
                               ps_gram[s % 2][:, 0:FC * UB].rearrange("p (f b) -> p f b", b=UB)
                               ).then_inc(s_gram, 1)

            def tail(t, u):
                if u == 5:
                    load_ctx(t - 1)
                if u == 9:
                    act.wait_ge(s_gram, UNITS * CHUNKS * t)
                    nc.scalar.copy(sum2[:, :], gram[:, FIELDS, :]).then_inc(s_sum2, 1)
                if u == L3_SLOT + len(L3_FIELDS) + 1:
                    act.wait_ge(s_l3, t)
                    nc.scalar.copy(sum3[:, :], ps_mlp[:, 0:P]).then_inc(s_sum3, 1)
                if u == H1_SLOTS[-1] + 2:
                    act.wait_ge(s_h1_ps, t)
                    for m in range(HID1 // P):
                        ins = nc.scalar.activation(h1[:, m, :], ps_mlp[:, P * m:P * m + P],
                                                   ACT.Relu, bias=b1[:, m:m + 1])
                    ins.then_inc(s_h1, 1)
                if u == H2_SLOTS[-1] + 2:
                    act.wait_ge(s_h2_ps, t)
                    for m in range(HID2 // P):
                        ins = nc.scalar.activation(h2[:, m, :], ps_mlp[:, P * m:P * m + P],
                                                   ACT.Relu, bias=b2[:, m:m + 1])
                    ins.then_inc(s_h2, 1)
                if u == Y_SLOT + 3:
                    act.wait_ge(s_y_ps, t)
                    act.wait_ge(s_out, LAND * t)
                    nc.scalar.copy(y[:, :], ps_mlp[0:1, 0:P]).then_inc(s_y, 1)
                    act.wait_ge(s_y, t)
                    act.dma_start(out_t[t - 1], y[:, :]).then_inc(s_out, LAND)

            def tile(t, first=False, last=False, gathers=True):
                for u in range(TSLOTS):
                    c, k = u // SLOTS, u % SLOTS
                    round_z(t, u, last)
                    if gathers and u == IDS_SLOT:
                        load_early(t + 2)
                    if gathers and u == GATHER_SLOT:
                        load_late(t + 2)
                    if k == 1 and u > 1:
                        take_x2(t, c - 1)
                    if u == 1 and not first:
                        take_x2(t - 1, CHUNKS - 1)
                    for work in front_at(t, c, k, last):
                        front(*work)
                    if not last and u == STAGE_SLOT:
                        stage(t + 1)
                    if last and u == TSLOTS - 1:
                        spread_fields(t, c, range(UB))
                    if not (first and c == 0):
                        unit_work(*before(t, c), k)
                        for s in blocks_at(gram_slots((c - 1) % CHUNKS), k - 2):
                            take_gram(*before(t, c), s)
                    if not first:
                        tail(t, u)

            act.nop().then_inc(s_out, LAND)
            act.wait_ge(s_masks, LAND * 2)
            act.wait_ge(s_ones, 1)
            act.wait_ge(s_w1, LAND)
            nc.scalar.copy(wh[:, :, :].rearrange("p a b -> p (a b)"),
                           gram[:, 0:FIELDS, :].rearrange("p a b -> p (a b)")).then_inc(s_wh, 1)
            stage(0)
            front(0, 0, 0)
            front(0, 1, 0)
            load_early(1)
            load_late(1)
            front(0, 0, 11)
            tile(0, first=True)
            with act.Fori(1, TILES - 2) as t:
                tile(t)
            tile(TILES - 2, gathers=False)
            tile(TILES - 1, last=True, gathers=False)
            take_x2(TILES - 1, CHUNKS - 1)
            turn_x2(TILES - 1, CHUNKS - 1)
            for s in range(UNITS):
                take_gram(TILES - 1, CHUNKS - 1, s)
            for u in range(TSLOTS):
                tail(TILES, u)
            act.wait_ge(s_out, LAND * (TILES + 1))

        @block.vector
        def _(dve):
            def front(t, c, r):
                g = CHUNKS * t + c
                if 3 <= r < 3 + PAIRS:
                    i = r - 3
                    dve.wait_ge(*pair_sem(t, c, i))
                    if i == 0:
                        dve.wait_ge(s_same, LAND * (g + 1))
                    nc.vector.tensor_tensor(pair_group(t, c, i), pair_group(t, c, i),
                                            x0_same[:, :], ALU.mult).then_inc(s_z1, 1)
                if r == 12:
                    dve.wait_ge(s_x1, g + 1)
                    if c == 0:
                        wait(dve, s_sum1, t)
                    nc.vector.tensor_reduce(sum1_next[:, CHUNK_B * c:CHUNK_B * c + CHUNK_B],
                                            x1[:, :].rearrange("p (b i) -> p b i", i=DIM),
                                            AX_X, ALU.add).then_inc(s_sums, 1)

            def products(t, c, k):
                u = SLOTS * c + k
                j = TSLOTS * t + u
                g = CHUNKS * t + c
                if k == 0:
                    dve.wait_ge(s_x1, g + 1)
                if k == 1:
                    dve.wait_ge(s_x1q, LAND * (g + 1))
                blocks = range(FIRST) if k == 0 else (FIRST - 1 + k,)
                for v in blocks:
                    dve.wait_ge(s_spread[v % SPREADS], spread_wait(t, c, v))
                wait(dve, s_zh, 2 * (j - 1))
                wait(dve, s_zl_pool, j - 1)
                wait(dve, s_zl_dve, j - 1)
                n = blocks_of(k)
                out = z[:, k % 2, 0:N * n].rearrange("p (i n) -> p i n", n=N)
                if k == 0:
                    nc.vector.tensor_tensor(out, x0_spread[:, 0:n, :],
                                            x1[:, None, :].broadcast_to([P, n, N]),
                                            ALU.mult).then_inc(s_z, 1)
                else:
                    nc.vector.tensor_tensor(out,
                                            x0_spread[:, blocks[0] % SPREADS, None, :
                                                      ].broadcast_to([P, n, N]),
                                            x1q[:, c % 2, :, :], ALU.mult).then_inc(s_z, 1)

            def rest(t, u, last=False):
                j = TSLOTS * t + u
                dve.wait_ge(s_zh, 2 * j + 2)
                wait(dve, s_l2, j - 1)
                n, end = pool_cols(u, last), N * blocks_of(u % SLOTS)
                nc.vector.tensor_tensor(zl[:, u % 2, n:end], z[:, u % 2, n:end],
                                        zh[:, u % HIGHS, n:end].bitcast(F32), ALU.subtract
                                        ).then_inc(s_zl_dve, 1)

            def move_sums(t):
                wait(dve, s_h1_ps, t)
                dve.wait_ge(s_sums, CHUNKS * t + CHUNKS)
                nc.vector.tensor_copy(sum1[:, :], sum1_next[:, :]).then_inc(s_sum1, 1)

            def tile(t, first=False, last=False):
                for u in range(TSLOTS):
                    c, k = u // SLOTS, u % SLOTS
                    if u + 1 < TSLOTS:
                        products(t, (u + 1) // SLOTS, (u + 1) % SLOTS)
                    elif not last:
                        products(t + 1, 0, 0)
                    if not (first and u == 0):
                        rest(t, u, last)
                    if u == 35:
                        move_sums(t)
                    for work in front_at(t, c, k, last):
                        front(*work)

            dve.wait_ge(s_masks, LAND * 2)
            nc.vector.tensor_copy(diag[:, :, FIELDS, :],
                                  mask[:, None, :].broadcast_to([P, UNITS, UB])
                                  ).then_inc(s_ones, 1)
            dve.wait_ge(s_w0, LAND * 2)
            nc.vector.tensor_tensor(ws[:, :, :].rearrange("p i m -> p (i m)"),
                                    ws[:, :, :].rearrange("p i m -> p (i m)"),
                                    w0_lower, ALU.add).then_inc(s_ws, 1)
            dve.wait_ge(s_wh, 1)
            nc.vector.tensor_tensor(wl[:, :, :].rearrange("p a b -> p (a b)"),
                                    gram[:, 0:FIELDS, :].rearrange("p a b -> p (a b)"),
                                    wh[:, :, :].rearrange("p a b -> p (a b)").bitcast(F32),
                                    ALU.subtract).then_inc(s_wl, 1)
            for r in range(12):
                front(0, 0, r)
            products(0, 0, 0)
            front(0, 0, 12)
            for r in range(START):
                front(0, 1, r)
            rest(0, 0)
            for r in range(START, SLOTS - FRONT):
                front(0, 1, r)
            tile(0, first=True)
            with dve.Fori(1, TILES - 1) as t:
                tile(t)
            tile(TILES - 1, last=True)


def kernel(**inputs):
    import numpy as np
    import concourse.bacc as bacc
    from concourse.bass_utils import run_bass_kernel_spmd as run

    nc = bacc.Bacc("TRN2", target_bir_lowering=False, num_devices=1,
                   dynamic_dma_scratch_size=8192)

    def pair_rows(w):
        w = w.reshape(FIELDS, FIELDS, P)
        f = np.arange(FIELDS)
        upper, lower = (np.zeros((PAIRS * DELTAS, FIELDS, P), w.dtype) for _ in range(2))
        for delta in range(PAIRS * DELTAS):
            g = (f + delta) % FIELDS
            upper[delta] = w[f, g]
            if 0 < delta < 19:
                lower[delta] = w[g, f]
        return [x.reshape(PAIRS, DELTAS, FIELDS, P).transpose(2, 1, 0, 3).reshape(ROWS, PAIRS, P)
                for x in (upper, lower)]

    def slot_rows(w):
        w = w.reshape(FIELDS, P, P)
        rest = w[FIRST:].reshape(SLOTS - 1, QUADS, QP, 4, P).transpose(2, 1, 0, 3, 4)
        return np.concatenate([w[:FIRST].transpose(1, 0, 2), rest.reshape(P, -1, P)], axis=1)

    upper, lower = pair_rows(np.asarray(inputs["L0_rec_f0"]))
    arrays = {
        "ids": np.asarray(inputs["ids"]),
        "ctxt": np.asarray(inputs["dense_ctx"]).reshape(TILES, P, CTX).transpose(0, 2, 1),
        "wu": upper, "wl": lower,
        "w1": slot_rows(np.asarray(inputs["L0_rec_f1"])),
        "w2": np.asarray(inputs["L0_rec_f2"]).reshape(FIELDS, P, P).transpose(1, 0, 2),
        "top1": np.asarray(inputs["W_top1"]),
        "b1": np.asarray(inputs["b_top1"]).reshape(HID1 // P, P).T,
        "top2": np.asarray(inputs["W_top2"]),
        "b2": np.asarray(inputs["b_top2"]).reshape(HID2 // P, P).T,
        "top3": np.asarray(inputs["W_top3"]).reshape(HID2 // P, P).T,
        "ident": np.eye(P, dtype=np.float32),
        "mask": np.repeat(np.eye(UB, dtype=np.float32), DIM, axis=0),
    }
    for f in range(FIELDS):
        arrays[f"tbl_{f}"] = np.asarray(inputs[f"tbl_{f}"])
    arrays = {f"in_{k}": np.ascontiguousarray(a) for k, a in arrays.items()}
    ap = {k[3:]: nc.dram_tensor(k, a.shape, mybir.dt.from_np(a.dtype), kind="ExternalInput").ap()
          for k, a in arrays.items()}
    x0_dram = nc.dram_tensor("x0_dram", (CHUNKS, FIELDS + WRAP, N), F32, kind="Internal").ap()
    x1_dram = nc.dram_tensor("x1_dram", (P, N), F32, kind="Internal").ap()
    out = nc.dram_tensor("out", (BATCH, 1), F32, kind="ExternalOutput").ap()
    build(nc, ap["ids"], [ap[f"tbl_{f}"] for f in range(FIELDS)], ap["ctxt"], ap["wu"], ap["wl"],
          ap["w1"], ap["w2"], ap["top1"], ap["b1"], ap["top2"], ap["b2"], ap["top3"], 
          ap["ident"], ap["mask"], x0_dram, x1_dram, out)
    return run(nc, [arrays], core_ids=[0]).results[0]["out"]
```
